# Optimizing a Trainium2 kernel written in Bass

```python
import numpy as np
import jax
import jax.numpy as jnp

def _softmax(x, axis=-1):
    return jax.nn.softmax(x, axis=axis)

def _gelu(x):
    return jax.nn.gelu(x, approximate=True)

def _silu(x):
    return jax.nn.silu(x)

def _sigmoid(x):
    return jax.nn.sigmoid(x)

def _layernorm(x, axis=-1, eps=1e-05):
    m = jnp.mean(x, axis=axis, keepdims=True)
    v = jnp.var(x, axis=axis, keepdims=True)
    return (x - m) / jnp.sqrt(v + eps)

def _scatter_add(tgt, idx, src, axis=0):
    return tgt.at[idx].add(src)

def _segment_sum(src, seg, n):
    return jax.ops.segment_sum(src, seg, n)
kernel_name = 'mk_audio_tower_d4_tok_audfeat512_r4_236fba'

def setup_inputs(seed: int=0):
    np.random.seed(seed)
    _w = jnp.asarray

    def _rec_inputs():
        import jax
        import jax.numpy as jnp
        _rk = jax.random.key(seed)
        x = -3.53888e-05 + 1.00021 * jax.random.normal(jax.random.fold_in(_rk, 1), (8, 375, 23), jnp.float32)
        return x
    x = _rec_inputs()

    def _L0_tok_setup():
        import jax, jax.numpy as jnp
        import numpy as np
        CONTEXT = 5
        DILATION = 1
        BN_EPS = 1e-05

        def _tdnn_forward(x, W, b, gamma, beta):
            B, T, D = x.shape
            L = T - (CONTEXT - 1) * DILATION
            frames = jnp.stack([jax.lax.dynamic_slice_in_dim(x, k * DILATION, L, axis=1) for k in range(CONTEXT)], axis=2)
            patches = frames.reshape(B, L, CONTEXT * D)
            y = jnp.einsum('blf,of->blo', patches, W) + b
            y = jax.nn.relu(y)
            mean = jnp.mean(y, axis=(0, 1))
            var = jnp.var(y, axis=(0, 1))
            y = (y - mean) * jax.lax.rsqrt(var + BN_EPS) * gamma + beta
            return y
        key = jax.random.key(seed)
        k1, k2, k3 = jax.random.split(key, 3)
        B, T, D, O = (64, 1024, 23, 128)
        x = jax.random.normal(k1, (B, T, D), dtype=jnp.float32)
        fan_in = D * CONTEXT
        bound = 1.0 / np.sqrt(fan_in)
        W = jax.random.uniform(k2, (O, fan_in), dtype=jnp.float32, minval=-bound, maxval=bound)
        b = jax.random.uniform(k3, (O,), dtype=jnp.float32, minval=-bound, maxval=bound)
        gamma = jnp.ones((O,), dtype=jnp.float32)
        beta = jnp.zeros((O,), dtype=jnp.float32)
        return {'x': x, 'W': W, 'b': b, 'gamma': gamma, 'beta': beta}
    _L0_tok_all = _L0_tok_setup()
    _L0_tok_in = {k: v for k, v in _L0_tok_all.items() if k in ('W', 'b', 'gamma', 'beta')}
    del _L0_tok_all

    def _L0_attn_setup():
        import jax, jax.numpy as jnp
        import numpy as np
        from jax import lax
        B, S, D = (4, 512, 128)
        H, DK, DV, DH = (8, 64, 64, 64)
        KCONV = 4
        LN_EPS = 1e-05

        def _mlp(x, W2, W1, residual):
            h = jax.nn.silu(x @ W2.T) @ W1.T
            return x + h if residual else h

        def _ln(x, g, b):
            mu = jnp.mean(x, axis=-1, keepdims=True)
            var = jnp.mean(jnp.square(x - mu), axis=-1, keepdims=True)
            return (x - mu) * jax.lax.rsqrt(var + LN_EPS) * g + b
        key = jax.random.key(seed)
        ks = jax.random.split(key, 20)
        sc = 0.02
        return {'x': jax.random.normal(ks[0], (B, S, D), jnp.float32), 'conv_w': jax.random.normal(ks[1], (D, 1, KCONV), jnp.float32) * sc, 'conv_b': jnp.zeros((D,), jnp.float32), 'Wq': jax.random.normal(ks[2], (H * DK, D), jnp.float32) * sc, 'Mk_W2': jax.random.normal(ks[3], (DH, D), jnp.float32) * sc, 'Mk_W1': jax.random.normal(ks[4], (H * DK, DH), jnp.float32) * sc, 'Mv_W2': jax.random.normal(ks[5], (DH, D), jnp.float32) * sc, 'Mv_W1': jax.random.normal(ks[6], (H * DV, DH), jnp.float32) * sc, 'Meta_W2': jax.random.normal(ks[7], (DH, D), jnp.float32) * sc, 'Meta_W1': jax.random.normal(ks[8], (H, DH), jnp.float32) * sc, 'Malpha_W2': jax.random.normal(ks[9], (DH, D), jnp.float32) * sc, 'Malpha_W1': jax.random.normal(ks[10], (H, DH), jnp.float32) * sc, 'Mvh_W2': jax.random.normal(ks[11], (DH, H * DV), jnp.float32) * sc, 'Mvh_W1': jax.random.normal(ks[12], (H * DV, DH), jnp.float32) * sc, 'normk_g': jnp.ones((H * DK,), jnp.float32), 'normk_b': jnp.zeros((H * DK,), jnp.float32), 'normq_g': jnp.ones((H * DK,), jnp.float32), 'normq_b': jnp.zeros((H * DK,), jnp.float32), 'out_W': jax.random.normal(ks[13], (D, H * DV), jnp.float32) * sc, 'out_b': jnp.zeros((D,), jnp.float32)}
    _L0_attn_all = _L0_attn_setup()
    _L0_attn_in = {k: v for k, v in _L0_attn_all.items() if k in ('conv_w', 'conv_b', 'Wq', 'Mk_W2', 'Mk_W1', 'Mv_W2', 'Mv_W1', 'Meta_W2', 'Meta_W1', 'Malpha_W2', 'Malpha_W1', 'Mvh_W2', 'Mvh_W1', 'normk_g', 'normk_b', 'normq_g', 'normq_b', 'out_W', 'out_b')}
    del _L0_attn_all

    def _L0_ffn_setup():
        import jax, jax.numpy as jnp
        import numpy as np
        B, S, D = (4, 512, 128)
        I = 96
        E = 16
        K = 2

        def _inv_softplus(v):
            return float(np.log(np.expm1(v)))

        def swiglu5(h, alpha, gate_scale, up_shift, gate_clamp_raw, up_clamp_raw):
            gate_clamp = jax.nn.softplus(gate_clamp_raw)
            up_clamp = jax.nn.softplus(up_clamp_raw)
            g = jnp.clip(h[..., ::2], -gate_clamp, gate_clamp)
            u = jnp.clip(h[..., 1::2], -up_clamp, up_clamp)
            return g * jax.nn.sigmoid(g * alpha) * gate_scale * (u + up_shift)
        key = jax.random.key(seed)
        ks = jax.random.split(key, 10)
        std = 0.02
        raw = _inv_softplus(7.0)
        act = jnp.array([1.702, 1.0, 1.0, raw, raw], dtype=jnp.float32)
        return {'x': jax.random.normal(ks[0], (B, S, D), dtype=jnp.float32), 'gate_w': jax.random.normal(ks[1], (D, E), dtype=jnp.float32) * 0.01, 'gate_b': jnp.zeros((E,), dtype=jnp.float32), 'shared_w1': jax.random.normal(ks[2], (D, 2 * I), dtype=jnp.float32) * std, 'shared_b1': jnp.zeros((2 * I,), dtype=jnp.float32), 'shared_w2': jax.random.normal(ks[3], (I, D), dtype=jnp.float32) * std, 'shared_b2': jnp.zeros((D,), dtype=jnp.float32), 'shared_act': act, 'expert_w1': jax.random.normal(ks[4], (E, D, 2 * I), dtype=jnp.float32) * std, 'expert_b1': jnp.zeros((E, 2 * I), dtype=jnp.float32), 'expert_w2': jax.random.normal(ks[5], (E, I, D), dtype=jnp.float32) * std, 'expert_b2': jnp.zeros((E, D), dtype=jnp.float32), 'expert_act': jnp.tile(act[None, :], (E, 1))}
    _L0_ffn_all = _L0_ffn_setup()
    _L0_ffn_in = {k: v for k, v in _L0_ffn_all.items() if k in ('gate_w', 'gate_b', 'shared_w1', 'shared_b1', 'shared_w2', 'shared_b2', 'shared_act', 'expert_w1', 'expert_b1', 'expert_w2', 'expert_b2', 'expert_act')}
    del _L0_ffn_all

    def _L1_attn_setup():
        import jax, jax.numpy as jnp
        import numpy as np
        B, N, DIN, DINNER, DOUT, W = (4, 2048, 128, 128, 128, 128)
        key = jax.random.key(seed)
        k1, k2, k3 = jax.random.split(key, 3)
        x = jax.random.normal(k1, (B, N, DIN), jnp.float32)
        w_qkv = jax.random.normal(k2, (3 * DINNER, DIN), jnp.float32) * DIN ** (-0.5)
        w_out = jax.random.normal(k3, (DOUT, DINNER), jnp.float32) * DINNER ** (-0.5)
        b_out = jnp.zeros((DOUT,), jnp.float32)
        return {'x': x, 'w_qkv': w_qkv, 'w_out': w_out, 'b_out': b_out}
    _L1_attn_all = _L1_attn_setup()
    _L1_attn_in = {k: v for k, v in _L1_attn_all.items() if k in ('w_qkv', 'w_out', 'b_out')}
    del _L1_attn_all

    def _L1_ffn_setup():
        import jax, jax.numpy as jnp
        import numpy as np
        D = 128
        F = 512
        E = 8
        K = 2
        B, S = (2, 1024)
        key = jax.random.key(seed)
        ks = jax.random.split(key, 8)
        sd = 1.0 / np.sqrt(D)
        sf = 1.0 / np.sqrt(F)
        return {'x': jax.random.normal(ks[0], (B, S, D), dtype=jnp.float32), 'router_w': jax.random.uniform(ks[1], (D, E), jnp.float32, -sd, sd), 'router_b': jax.random.uniform(ks[2], (E,), jnp.float32, -sd, sd), 'w1': jax.random.uniform(ks[3], (E, D, F), jnp.float32, -sd, sd), 'b1': jax.random.uniform(ks[4], (E, F), jnp.float32, -sd, sd), 'w2': jax.random.uniform(ks[5], (E, F, D), jnp.float32, -sf, sf), 'b2': jax.random.uniform(ks[6], (E, D), jnp.float32, -sf, sf)}
    _L1_ffn_all = _L1_ffn_setup()
    _L1_ffn_in = {k: v for k, v in _L1_ffn_all.items() if k in ('router_w', 'router_b', 'w1', 'b1', 'w2', 'b2')}
    del _L1_ffn_all

    def _L2_attn_setup():
        import jax, jax.numpy as jnp
        import numpy as np
        NUM_HEADS = 8
        key = jax.random.key(seed)
        k1, k2, k3 = jax.random.split(key, 3)
        B, N, C = (4, 512, 128)
        x = jax.random.normal(k1, (B, N, C), dtype=jnp.float32)
        q_w = jax.random.normal(k2, (C, C), dtype=jnp.float32) * 0.02
        kv_w = jax.random.normal(k3, (2 * C, C), dtype=jnp.float32) * 0.02
        return {'x': x, 'q_w': q_w, 'kv_w': kv_w}
    _L2_attn_all = _L2_attn_setup()
    _L2_attn_in = {k: v for k, v in _L2_attn_all.items() if k in ('q_w', 'kv_w')}
    del _L2_attn_all

    def _L2_ffn_setup():
        import jax, jax.numpy as jnp
        import numpy as np
        B, S, D, F, E, K = (4, 512, 128, 512, 8, 2)
        key = jax.random.key(seed)
        kx, kg, kw, kv, k2 = jax.random.split(key, 5)
        scale = 0.02
        return {'x': jax.random.normal(kx, (B, S, D), dtype=jnp.float32), 'Wg': jax.random.normal(kg, (D, E), dtype=jnp.float32) * scale, 'W': jax.random.normal(kw, (E, D, F), dtype=jnp.float32) * scale, 'V': jax.random.normal(kv, (E, D, F), dtype=jnp.float32) * scale, 'W2': jax.random.normal(k2, (E, F, D), dtype=jnp.float32) * scale}
    _L2_ffn_all = _L2_ffn_setup()
    _L2_ffn_in = {k: v for k, v in _L2_ffn_all.items() if k in ('Wg', 'W', 'V', 'W2')}
    del _L2_ffn_all

    def _L3_attn_setup():
        import jax, jax.numpy as jnp
        import numpy as np
        EPS = 1e-05
        NUM_HEADS = 8
        SCALE = 0.125

        def _lin_bn_relu(x, w, b, g, beta, mu, var):
            y = jnp.einsum('bnc,dc->bnd', x, w) + b
            y = (y - mu) * (g / jnp.sqrt(var + EPS)) + beta
            return jax.nn.relu(y)
        key = jax.random.key(seed)
        B, N, C = (8, 256, 128)
        keys = jax.random.split(key, 16)
        d = {'x': jax.random.normal(keys[0], (B, N, C), dtype=jnp.float32)}
        for i, p in enumerate(['q', 'k', 'v', 'p']):
            kw, kb, kmu = (keys[1 + 3 * i], keys[2 + 3 * i], keys[3 + 3 * i])
            d[f'{p}_w'] = jax.random.normal(kw, (C, C), dtype=jnp.float32) * 0.02
            d[f'{p}_b'] = jnp.zeros((C,), dtype=jnp.float32)
            d[f'{p}_g'] = jnp.ones((C,), dtype=jnp.float32)
            d[f'{p}_beta'] = jnp.zeros((C,), dtype=jnp.float32)
            d[f'{p}_mu'] = jax.random.normal(kmu, (C,), dtype=jnp.float32) * 0.02
            d[f'{p}_var'] = jax.random.uniform(kb, (C,), dtype=jnp.float32, minval=0.5, maxval=1.5)
        return d
    _L3_attn_all = _L3_attn_setup()
    _L3_attn_in = {k: v for k, v in _L3_attn_all.items() if k in ('q_w', 'q_b', 'q_g', 'q_beta', 'q_mu', 'q_var', 'k_w', 'k_b', 'k_g', 'k_beta', 'k_mu', 'k_var', 'v_w', 'v_b', 'v_g', 'v_beta', 'v_mu', 'v_var', 'p_w', 'p_b', 'p_g', 'p_beta', 'p_mu', 'p_var')}
    del _L3_attn_all

    def _L3_ffn_setup():
        import jax, jax.numpy as jnp
        import numpy as np
        DIM = 128
        HID = 256
        E = 8
        K = 2
        B, S = (4, 512)
        key = jax.random.key(seed)
        ks = jax.random.split(key, 10)
        sd = DIM ** (-0.5)
        sh = HID ** (-0.5)
        return {'x': jax.random.normal(ks[0], (B, S, DIM), dtype=jnp.float32), 'gate_w': jax.random.normal(ks[1], (E, DIM), dtype=jnp.float32) * sd, 'biases': jnp.zeros((E,), dtype=jnp.float32), 'w1': jax.random.normal(ks[2], (E, DIM, HID), dtype=jnp.float32) * sd, 'w3': jax.random.normal(ks[3], (E, DIM, HID), dtype=jnp.float32) * sd, 'w2': jax.random.normal(ks[4], (E, HID, DIM), dtype=jnp.float32) * sh, 'sw1': jax.random.normal(ks[5], (DIM, HID), dtype=jnp.float32) * sd, 'sw3': jax.random.normal(ks[6], (DIM, HID), dtype=jnp.float32) * sd, 'sw2': jax.random.normal(ks[7], (HID, DIM), dtype=jnp.float32) * sh}
    _L3_ffn_all = _L3_ffn_setup()
    _L3_ffn_in = {k: v for k, v in _L3_ffn_all.items() if k in ('gate_w', 'biases', 'w1', 'w3', 'w2', 'sw1', 'sw3', 'sw2')}
    del _L3_ffn_all
    return {'x': x, 'L0_tok_W': _L0_tok_in['W'], 'L0_tok_b': _L0_tok_in['b'], 'L0_tok_gamma': _L0_tok_in['gamma'], 'L0_tok_beta': _L0_tok_in['beta'], 'L0_attn_conv_w': _L0_attn_in['conv_w'], 'L0_attn_conv_b': _L0_attn_in['conv_b'], 'L0_attn_Wq': _L0_attn_in['Wq'], 'L0_attn_Mk_W2': _L0_attn_in['Mk_W2'], 'L0_attn_Mk_W1': _L0_attn_in['Mk_W1'], 'L0_attn_Mv_W2': _L0_attn_in['Mv_W2'], 'L0_attn_Mv_W1': _L0_attn_in['Mv_W1'], 'L0_attn_Meta_W2': _L0_attn_in['Meta_W2'], 'L0_attn_Meta_W1': _L0_attn_in['Meta_W1'], 'L0_attn_Malpha_W2': _L0_attn_in['Malpha_W2'], 'L0_attn_Malpha_W1': _L0_attn_in['Malpha_W1'], 'L0_attn_Mvh_W2': _L0_attn_in['Mvh_W2'], 'L0_attn_Mvh_W1': _L0_attn_in['Mvh_W1'], 'L0_attn_normk_g': _L0_attn_in['normk_g'], 'L0_attn_normk_b': _L0_attn_in['normk_b'], 'L0_attn_normq_g': _L0_attn_in['normq_g'], 'L0_attn_normq_b': _L0_attn_in['normq_b'], 'L0_attn_out_W': _L0_attn_in['out_W'], 'L0_attn_out_b': _L0_attn_in['out_b'], 'L0_ffn_gate_w': _L0_ffn_in['gate_w'], 'L0_ffn_gate_b': _L0_ffn_in['gate_b'], 'L0_ffn_shared_w1': _L0_ffn_in['shared_w1'], 'L0_ffn_shared_b1': _L0_ffn_in['shared_b1'], 'L0_ffn_shared_w2': _L0_ffn_in['shared_w2'], 'L0_ffn_shared_b2': _L0_ffn_in['shared_b2'], 'L0_ffn_shared_act': _L0_ffn_in['shared_act'], 'L0_ffn_expert_w1': _L0_ffn_in['expert_w1'], 'L0_ffn_expert_b1': _L0_ffn_in['expert_b1'], 'L0_ffn_expert_w2': _L0_ffn_in['expert_w2'], 'L0_ffn_expert_b2': _L0_ffn_in['expert_b2'], 'L0_ffn_expert_act': _L0_ffn_in['expert_act'], 'L1_attn_w_qkv': _L1_attn_in['w_qkv'], 'L1_attn_w_out': _L1_attn_in['w_out'], 'L1_attn_b_out': _L1_attn_in['b_out'], 'L1_ffn_router_w': _L1_ffn_in['router_w'], 'L1_ffn_router_b': _L1_ffn_in['router_b'], 'L1_ffn_w1': _L1_ffn_in['w1'], 'L1_ffn_b1': _L1_ffn_in['b1'], 'L1_ffn_w2': _L1_ffn_in['w2'], 'L1_ffn_b2': _L1_ffn_in['b2'], 'L2_attn_q_w': _L2_attn_in['q_w'], 'L2_attn_kv_w': _L2_attn_in['kv_w'], 'L2_ffn_Wg': _L2_ffn_in['Wg'], 'L2_ffn_W': _L2_ffn_in['W'], 'L2_ffn_V': _L2_ffn_in['V'], 'L2_ffn_W2': _L2_ffn_in['W2'], 'L3_attn_q_w': _L3_attn_in['q_w'], 'L3_attn_q_b': _L3_attn_in['q_b'], 'L3_attn_q_g': _L3_attn_in['q_g'], 'L3_attn_q_beta': _L3_attn_in['q_beta'], 'L3_attn_q_mu': _L3_attn_in['q_mu'], 'L3_attn_q_var': _L3_attn_in['q_var'], 'L3_attn_k_w': _L3_attn_in['k_w'], 'L3_attn_k_b': _L3_attn_in['k_b'], 'L3_attn_k_g': _L3_attn_in['k_g'], 'L3_attn_k_beta': _L3_attn_in['k_beta'], 'L3_attn_k_mu': _L3_attn_in['k_mu'], 'L3_attn_k_var': _L3_attn_in['k_var'], 'L3_attn_v_w': _L3_attn_in['v_w'], 'L3_attn_v_b': _L3_attn_in['v_b'], 'L3_attn_v_g': _L3_attn_in['v_g'], 'L3_attn_v_beta': _L3_attn_in['v_beta'], 'L3_attn_v_mu': _L3_attn_in['v_mu'], 'L3_attn_v_var': _L3_attn_in['v_var'], 'L3_attn_p_w': _L3_attn_in['p_w'], 'L3_attn_p_b': _L3_attn_in['p_b'], 'L3_attn_p_g': _L3_attn_in['p_g'], 'L3_attn_p_beta': _L3_attn_in['p_beta'], 'L3_attn_p_mu': _L3_attn_in['p_mu'], 'L3_attn_p_var': _L3_attn_in['p_var'], 'L3_ffn_gate_w': _L3_ffn_in['gate_w'], 'L3_ffn_biases': _L3_ffn_in['biases'], 'L3_ffn_w1': _L3_ffn_in['w1'], 'L3_ffn_w3': _L3_ffn_in['w3'], 'L3_ffn_w2': _L3_ffn_in['w2'], 'L3_ffn_sw1': _L3_ffn_in['sw1'], 'L3_ffn_sw3': _L3_ffn_in['sw3'], 'L3_ffn_sw2': _L3_ffn_in['sw2']}

def reference(x, L0_tok_W, L0_tok_b, L0_tok_gamma, L0_tok_beta, L0_attn_conv_w, L0_attn_conv_b, L0_attn_Wq, L0_attn_Mk_W2, L0_attn_Mk_W1, L0_attn_Mv_W2, L0_attn_Mv_W1, L0_attn_Meta_W2, L0_attn_Meta_W1, L0_attn_Malpha_W2, L0_attn_Malpha_W1, L0_attn_Mvh_W2, L0_attn_Mvh_W1, L0_attn_normk_g, L0_attn_normk_b, L0_attn_normq_g, L0_attn_normq_b, L0_attn_out_W, L0_attn_out_b, L0_ffn_gate_w, L0_ffn_gate_b, L0_ffn_shared_w1, L0_ffn_shared_b1, L0_ffn_shared_w2, L0_ffn_shared_b2, L0_ffn_shared_act, L0_ffn_expert_w1, L0_ffn_expert_b1, L0_ffn_expert_w2, L0_ffn_expert_b2, L0_ffn_expert_act, L1_attn_w_qkv, L1_attn_w_out, L1_attn_b_out, L1_ffn_router_w, L1_ffn_router_b, L1_ffn_w1, L1_ffn_b1, L1_ffn_w2, L1_ffn_b2, L2_attn_q_w, L2_attn_kv_w, L2_ffn_Wg, L2_ffn_W, L2_ffn_V, L2_ffn_W2, L3_attn_q_w, L3_attn_q_b, L3_attn_q_g, L3_attn_q_beta, L3_attn_q_mu, L3_attn_q_var, L3_attn_k_w, L3_attn_k_b, L3_attn_k_g, L3_attn_k_beta, L3_attn_k_mu, L3_attn_k_var, L3_attn_v_w, L3_attn_v_b, L3_attn_v_g, L3_attn_v_beta, L3_attn_v_mu, L3_attn_v_var, L3_attn_p_w, L3_attn_p_b, L3_attn_p_g, L3_attn_p_beta, L3_attn_p_mu, L3_attn_p_var, L3_ffn_gate_w, L3_ffn_biases, L3_ffn_w1, L3_ffn_w3, L3_ffn_w2, L3_ffn_sw1, L3_ffn_sw3, L3_ffn_sw2):
    import jax
    import jax.numpy as jnp

    def _L0_tok_ref(x, W, b, gamma, beta):
        import jax, jax.numpy as jnp
        import numpy as np
        CONTEXT = 5
        DILATION = 1
        BN_EPS = 1e-05

        def _tdnn_forward(x, W, b, gamma, beta):
            B, T, D = x.shape
            L = T - (CONTEXT - 1) * DILATION
            frames = jnp.stack([jax.lax.dynamic_slice_in_dim(x, k * DILATION, L, axis=1) for k in range(CONTEXT)], axis=2)
            patches = frames.reshape(B, L, CONTEXT * D)
            y = jnp.einsum('blf,of->blo', patches, W) + b
            y = jax.nn.relu(y)
            mean = jnp.mean(y, axis=(0, 1))
            var = jnp.var(y, axis=(0, 1))
            y = (y - mean) * jax.lax.rsqrt(var + BN_EPS) * gamma + beta
            return y
        return _tdnn_forward(x, W, b, gamma, beta)

    def _L0_attn_ref(x, conv_w, conv_b, Wq, Mk_W2, Mk_W1, Mv_W2, Mv_W1, Meta_W2, Meta_W1, Malpha_W2, Malpha_W1, Mvh_W2, Mvh_W1, normk_g, normk_b, normq_g, normq_b, out_W, out_b):
        import jax, jax.numpy as jnp
        import numpy as np
        from jax import lax
        B, S, D = (4, 512, 128)
        H, DK, DV, DH = (8, 64, 64, 64)
        KCONV = 4
        LN_EPS = 1e-05

        def _mlp(x, W2, W1, residual):
            h = jax.nn.silu(x @ W2.T) @ W1.T
            return x + h if residual else h

        def _ln(x, g, b):
            mu = jnp.mean(x, axis=-1, keepdims=True)
            var = jnp.mean(jnp.square(x - mu), axis=-1, keepdims=True)
            return (x - mu) * jax.lax.rsqrt(var + LN_EPS) * g + b
        b, s, d = x.shape
        xc = jnp.transpose(x, (0, 2, 1))
        yc = lax.conv_general_dilated(xc, conv_w, (1,), [(KCONV - 1, 0)], feature_group_count=d)
        x = x + jnp.transpose(yc + conv_b[None, :, None], (0, 2, 1))
        k = _ln(_mlp(x, Mk_W2, Mk_W1, False), normk_g, normk_b)
        v = _mlp(x, Mv_W2, Mv_W1, False)
        q = _ln(x @ Wq.T, normq_g, normq_b)
        eta = jax.nn.softplus(_mlp(x, Meta_W2, Meta_W1, False)) * 0.1
        alpha = jax.nn.sigmoid(_mlp(x, Malpha_W2, Malpha_W1, False))
        v_hat = _mlp(v, Mvh_W2, Mvh_W1, True)
        to_s = lambda t, dd: jnp.transpose(t.reshape(b, s, H, dd), (1, 0, 2, 3))
        q_s, k_s = (to_s(q, DK), to_s(k, DK))
        vh_s = to_s(v_hat, DV)
        eta_s = jnp.transpose(eta, (1, 0, 2))
        al_s = jnp.transpose(alpha, (1, 0, 2))
        eye = jnp.eye(DK, dtype=x.dtype)

        def step(mem, inp):
            q_t, k_t, vh_t, e_t, a_t = inp
            y_t = jnp.einsum('bhvk,bhk->bhv', mem, q_t)
            kn = k_t / jnp.maximum(jnp.linalg.norm(k_t, axis=-1, keepdims=True), 1e-12)
            err = jnp.einsum('bhvk,bhk->bhv', mem, kn) - vh_t
            e4 = e_t[:, :, None, None]
            a4 = a_t[:, :, None, None]
            decay = a4 * eye - e4 * (kn[:, :, :, None] * kn[:, :, None, :])
            mem = jnp.einsum('bhvk,bhkl->bhvl', mem, decay) - e4 * (err[:, :, :, None] * kn[:, :, None, :])
            return (mem, y_t)
        mem0 = jnp.zeros((b, H, DV, DK), x.dtype)
        _, ys = lax.scan(step, mem0, (q_s, k_s, vh_s, eta_s, al_s))
        out = jnp.transpose(ys, (1, 0, 2, 3)).reshape(b, s, H * DV)
        return out @ out_W.T + out_b

    def _L0_ffn_ref(x, gate_w, gate_b, shared_w1, shared_b1, shared_w2, shared_b2, shared_act, expert_w1, expert_b1, expert_w2, expert_b2, expert_act):
        import jax, jax.numpy as jnp
        import numpy as np
        B, S, D = (4, 512, 128)
        I = 96
        E = 16
        K = 2

        def _inv_softplus(v):
            return float(np.log(np.expm1(v)))

        def swiglu5(h, alpha, gate_scale, up_shift, gate_clamp_raw, up_clamp_raw):
            gate_clamp = jax.nn.softplus(gate_clamp_raw)
            up_clamp = jax.nn.softplus(up_clamp_raw)
            g = jnp.clip(h[..., ::2], -gate_clamp, gate_clamp)
            u = jnp.clip(h[..., 1::2], -up_clamp, up_clamp)
            return g * jax.nn.sigmoid(g * alpha) * gate_scale * (u + up_shift)
        shape = x.shape
        xf = x.reshape(-1, shape[-1])
        h = xf @ shared_w1 + shared_b1
        t = swiglu5(h, shared_act[0], shared_act[1], shared_act[2], shared_act[3], shared_act[4])
        z = t @ shared_w2 + shared_b2
        gate_logits = xf @ gate_w + gate_b
        gate_probs = jax.nn.softmax(gate_logits, -1)
        w, idx = jax.lax.top_k(gate_probs, K)
        w = w / jnp.sum(w, axis=-1, keepdims=True)
        cw = jnp.sum(jax.nn.one_hot(idx, E, dtype=xf.dtype) * w[..., None], axis=1)
        he = jnp.einsum('nd,edh->enh', xf, expert_w1) + expert_b1[:, None, :]
        a = expert_act
        te = swiglu5(he, a[:, 0, None, None], a[:, 1, None, None], a[:, 2, None, None], a[:, 3, None, None], a[:, 4, None, None])
        oe = jnp.einsum('enh,ehd->end', te, expert_w2) + expert_b2[:, None, :]
        y = jnp.einsum('ne,end->nd', cw, oe)
        return (y + z).reshape(shape)

    def _L1_attn_ref(x, w_qkv, w_out, b_out):
        import jax, jax.numpy as jnp
        import numpy as np
        B, N, DIN, DINNER, DOUT, W = (4, 2048, 128, 128, 128, 128)
        b, n, _ = x.shape
        w = W
        scale = DINNER ** (-0.5)
        pad = -n % w
        xp = jnp.pad(x, ((0, 0), (0, pad), (0, 0)))
        qkv = jnp.einsum('bnd,ed->bne', xp, w_qkv)
        q, k, v = jnp.split(qkv, 3, axis=-1)
        win = lambda t: t.reshape(b, -1, w, DINNER)
        q, k, v = (win(q), win(k), win(v))
        kp = jnp.pad(k, ((0, 0), (1, 0), (0, 0), (0, 0)))
        k2 = jnp.concatenate((kp[:, :-1], kp[:, 1:]), axis=2)
        v2 = jnp.concatenate((kp[:, :-1], kp[:, 1:]), axis=2)
        sim = jnp.einsum('bwid,bwjd->bwij', q, k2) * scale
        i, j = (w, 2 * w)
        mask = jnp.triu(jnp.ones((i, j), bool), j - i + 1)
        sim = jnp.where(mask, -jnp.finfo(sim.dtype).max, sim)
        attn = jax.nn.softmax(sim, axis=-1)
        out = jnp.einsum('bwij,bwjd->bwid', attn, v2)
        out = out.reshape(b, -1, DINNER)[:, :n]
        return jnp.einsum('bnd,od->bno', out, w_out) + b_out

    def _L1_ffn_ref(x, router_w, router_b, w1, b1, w2, b2):
        import jax, jax.numpy as jnp
        import numpy as np
        D = 128
        F = 512
        E = 8
        K = 2
        B, S = (2, 1024)
        orig_shape = x.shape
        flat = x.reshape(-1, orig_shape[-1])
        logits = flat @ router_w + router_b
        gates = jax.nn.softmax(logits, axis=-1)
        top_vals, top_idx = jax.lax.top_k(gates, K)
        top_vals = top_vals / jnp.sum(top_vals, axis=-1, keepdims=True)
        onehot = jax.nn.one_hot(top_idx, E, dtype=flat.dtype)
        comb = jnp.einsum('tk,tke->te', top_vals, onehot)
        hidden = jax.nn.relu(jnp.einsum('td,edf->etf', flat, w1) + b1[:, None, :])
        eout = jnp.einsum('etf,efd->etd', hidden, w2) + b2[:, None, :]
        out = jnp.einsum('te,etd->td', comb, eout)
        return out.reshape(orig_shape)

    def _L2_attn_ref(x, q_w, kv_w):
        import jax, jax.numpy as jnp
        import numpy as np
        NUM_HEADS = 8
        B, N, C = x.shape
        H = NUM_HEADS
        D = C // H
        halfB = B // 2
        q = (x @ q_w.T).reshape(B, N, H, D)
        kv = (x @ kv_w.T).reshape(B, N, 2, H, D)
        k, v = (kv[:, :, 0], kv[:, :, 1])
        k = jnp.concatenate([k[halfB:], k[:halfB]], axis=0)
        v = jnp.concatenate([v[halfB:], v[:halfB]], axis=0)
        scores = jnp.einsum('bnhd,bmhd->bhnm', q, k) / jnp.sqrt(jnp.float32(C))
        prob = jax.nn.softmax(scores, axis=-1)
        out = jnp.einsum('bhnm,bmhd->bndh', prob, v).reshape(B, N, C)
        return out

    def _L2_ffn_ref(x, Wg, W, V, W2):
        import jax, jax.numpy as jnp
        import numpy as np
        B, S, D, F, E, K = (4, 512, 128, 512, 8, 2)
        gate_logits = jnp.einsum('bsd,de->bse', x, Wg)
        topv, topi = jax.lax.top_k(gate_logits, K)
        w = jax.nn.softmax(topv, axis=-1)
        gw = jnp.sum(w[..., None] * jax.nn.one_hot(topi, E, dtype=x.dtype), axis=-2)
        y = jnp.zeros_like(x)
        n_experts = W.shape[0]
        for e in range(n_experts):
            h = jax.nn.silu(jnp.einsum('bsd,df->bsf', x, W[e])) * jnp.einsum('bsd,df->bsf', x, V[e])
            y = y + gw[..., e:e + 1] * jnp.einsum('bsf,fd->bsd', h, W2[e])
        return y

    def _L3_attn_ref(x, q_w, q_b, q_g, q_beta, q_mu, q_var, k_w, k_b, k_g, k_beta, k_mu, k_var, v_w, v_b, v_g, v_beta, v_mu, v_var, p_w, p_b, p_g, p_beta, p_mu, p_var):
        import jax, jax.numpy as jnp
        import numpy as np
        EPS = 1e-05
        NUM_HEADS = 8
        SCALE = 0.125

        def _lin_bn_relu(x, w, b, g, beta, mu, var):
            y = jnp.einsum('bnc,dc->bnd', x, w) + b
            y = (y - mu) * (g / jnp.sqrt(var + EPS)) + beta
            return jax.nn.relu(y)
        B, N, C = x.shape
        H = NUM_HEADS
        dh = C // H

        def heads(t):
            return t.reshape(B, N, H, dh).transpose(0, 2, 1, 3)
        q = heads(_lin_bn_relu(x, q_w, q_b, q_g, q_beta, q_mu, q_var))
        k = heads(_lin_bn_relu(x, k_w, k_b, k_g, k_beta, k_mu, k_var))
        v = heads(_lin_bn_relu(x, v_w, v_b, v_g, v_beta, v_mu, v_var))
        attn = jnp.einsum('bhnd,bhmd->bhnm', q, k) * SCALE
        out = jnp.einsum('bhnm,bhmd->bhnd', attn, v)
        out = out.transpose(0, 2, 1, 3).reshape(B, N, C)
        out = jax.nn.relu(out)
        return _lin_bn_relu(out, p_w, p_b, p_g, p_beta, p_mu, p_var)

    def _L3_ffn_ref(x, gate_w, biases, w1, w3, w2, sw1, sw3, sw2):
        import jax, jax.numpy as jnp
        import numpy as np
        DIM = 128
        HID = 256
        E = 8
        K = 2
        B, S = (4, 512)
        Bb, Ss, D = x.shape
        xt = x.reshape(Bb * Ss, D)
        shared = jax.nn.silu(xt @ sw1) * (xt @ sw3) @ sw2
        scores = xt @ gate_w.T
        _, idx = jax.lax.top_k(scores + biases, K)
        topv, _ = jax.lax.top_k(scores, K)
        p = jax.nn.sigmoid(topv)
        p = p / jnp.sum(p, axis=-1, keepdims=True)
        h = jax.nn.silu(jnp.einsum('td,edh->eth', xt, w1)) * jnp.einsum('td,edh->eth', xt, w3)
        y = jnp.einsum('eth,ehd->etd', h, w2)
        onehot = jax.nn.one_hot(idx, E, dtype=xt.dtype)
        comb = jnp.einsum('tk,tke->te', p, onehot)
        out = jnp.einsum('te,etd->td', comb, y) + shared
        return out.reshape(Bb, Ss, D)
    h = _L0_tok_ref(x, L0_tok_W, L0_tok_b, L0_tok_gamma, L0_tok_beta)
    h = h + _L0_attn_ref(_layernorm(h, axis=-1), L0_attn_conv_w, L0_attn_conv_b, L0_attn_Wq, L0_attn_Mk_W2, L0_attn_Mk_W1, L0_attn_Mv_W2, L0_attn_Mv_W1, L0_attn_Meta_W2, L0_attn_Meta_W1, L0_attn_Malpha_W2, L0_attn_Malpha_W1, L0_attn_Mvh_W2, L0_attn_Mvh_W1, L0_attn_normk_g, L0_attn_normk_b, L0_attn_normq_g, L0_attn_normq_b, L0_attn_out_W, L0_attn_out_b)
    h = h + _L0_ffn_ref(_layernorm(h, axis=-1), L0_ffn_gate_w, L0_ffn_gate_b, L0_ffn_shared_w1, L0_ffn_shared_b1, L0_ffn_shared_w2, L0_ffn_shared_b2, L0_ffn_shared_act, L0_ffn_expert_w1, L0_ffn_expert_b1, L0_ffn_expert_w2, L0_ffn_expert_b2, L0_ffn_expert_act)
    h = h + _L1_attn_ref(_layernorm(h, axis=-1), L1_attn_w_qkv, L1_attn_w_out, L1_attn_b_out)
    h = h + _L1_ffn_ref(_layernorm(h, axis=-1), L1_ffn_router_w, L1_ffn_router_b, L1_ffn_w1, L1_ffn_b1, L1_ffn_w2, L1_ffn_b2)
    h = h + _L2_attn_ref(_layernorm(h, axis=-1), L2_attn_q_w, L2_attn_kv_w)
    h = h + _L2_ffn_ref(_layernorm(h, axis=-1), L2_ffn_Wg, L2_ffn_W, L2_ffn_V, L2_ffn_W2)
    h = h + _L3_attn_ref(_layernorm(h, axis=-1), L3_attn_q_w, L3_attn_q_b, L3_attn_q_g, L3_attn_q_beta, L3_attn_q_mu, L3_attn_q_var, L3_attn_k_w, L3_attn_k_b, L3_attn_k_g, L3_attn_k_beta, L3_attn_k_mu, L3_attn_k_var, L3_attn_v_w, L3_attn_v_b, L3_attn_v_g, L3_attn_v_beta, L3_attn_v_mu, L3_attn_v_var, L3_attn_p_w, L3_attn_p_b, L3_attn_p_g, L3_attn_p_beta, L3_attn_p_mu, L3_attn_p_var)
    h = h + _L3_ffn_ref(_layernorm(h, axis=-1), L3_ffn_gate_w, L3_ffn_biases, L3_ffn_w1, L3_ffn_w3, L3_ffn_w2, L3_ffn_sw1, L3_ffn_sw3, L3_ffn_sw2)
    return h

_drawn_inputs = setup_inputs


def setup_inputs(seed=0):
    import zlib

    import numpy as np

    out = dict(_drawn_inputs(seed))
    spreads = {'L0_tok_gamma': (1.0, 0.2),
     'L0_tok_beta': (0.0, 0.1),
     'L0_attn_conv_b': (0.0, 0.8),
     'L0_attn_normk_g': (1.0, 0.6),
     'L0_attn_normk_b': (0.0, 0.8),
     'L0_attn_normq_g': (1.0, 0.6),
     'L0_attn_normq_b': (0.0, 0.8),
     'L0_attn_out_b': (0.0, 0.41),
     'L0_ffn_gate_b': (0.0, 0.496),
     'L0_ffn_shared_b1': (0.0, 0.8),
     'L0_ffn_shared_b2': (0.0, 0.413),
     'L0_ffn_expert_b1': (0.0, 0.8),
     'L0_ffn_expert_b2': (0.0, 0.497),
     'L1_attn_b_out': (0.0, 0.405),
     'L3_attn_q_b': (0.0, 0.581),
     'L3_attn_q_g': (1.0, 0.6),
     'L3_attn_q_beta': (0.0, 0.8),
     'L3_attn_k_b': (0.0, 0.613),
     'L3_attn_k_g': (1.0, 0.6),
     'L3_attn_k_beta': (0.0, 0.8),
     'L3_attn_v_b': (0.0, 0.392),
     'L3_attn_v_g': (1.0, 0.6),
     'L3_attn_v_beta': (0.0, 0.321),
     'L3_attn_p_b': (0.0, 1.885),
     'L3_attn_p_g': (1.0, 0.6),
     'L3_attn_p_beta': (0.0, 0.628),
     'L3_ffn_biases': (0.0, 1.377)}
    factors = {'L0_attn_conv_w': 8.0,
     'L0_attn_Wq': 6.533,
     'L0_attn_Mk_W2': 6.353,
     'L0_attn_Mk_W1': 7.393,
     'L0_attn_Mv_W2': 8.0,
     'L0_attn_Mv_W1': 6.719,
     'L0_attn_Meta_W2': 8.0,
     'L0_attn_Meta_W1': 8.0,
     'L0_attn_Malpha_W2': 8.0,
     'L0_attn_Malpha_W1': 8.0,
     'L0_attn_Mvh_W2': 8.0,
     'L0_attn_Mvh_W1': 8.0,
     'L0_attn_out_W': 6.32,
     'L2_attn_q_w': 64.0,
     'L3_attn_q_mu': 24.056,
     'L0_ffn_gate_w': 4.744,
     'L0_ffn_shared_w1': 8.0,
     'L0_ffn_shared_w2': 8.0,
     'L0_ffn_expert_w1': 8.0,
     'L0_ffn_expert_w2': 8.0,
     'L1_ffn_router_b': 7.525,
     'L1_ffn_b1': 8.0,
     'L1_ffn_b2': 8.0,
     'L2_attn_kv_w': 3.602,
     'L2_ffn_Wg': 8.0,
     'L2_ffn_W': 8.0,
     'L2_ffn_V': 8.0,
     'L2_ffn_W2': 8.0,
     'L3_attn_q_w': 2.964,
     'L3_attn_q_var': 21.816,
     'L3_attn_k_w': 5.044,
     'L3_attn_k_mu': 8.0,
     'L3_attn_k_var': 8.0,
     'L3_attn_v_w': 3.485,
     'L3_attn_v_mu': 8.0,
     'L3_attn_v_var': 7.196,
     'L3_attn_p_mu': 64.0,
     'L3_attn_p_var': 5.023}
    for name, (base, spread) in spreads.items():
        noise = np.random.default_rng([zlib.crc32(name.encode()), seed]).standard_normal(out[name].shape)
        drawn = base * np.exp(spread * noise) if base else spread * noise
        out[name] = jnp.asarray(drawn.astype(out[name].dtype))
    for name, factor in factors.items():
        out[name] = (out[name] * factor).astype(out[name].dtype)
    return out
```

```python
from contextlib import ExitStack

import concourse.bass as bass
from concourse import mybir

F32 = mybir.dt.float32
BF16 = mybir.dt.bfloat16
U32 = mybir.dt.uint32
ALU = mybir.AluOpType
ACT = mybir.ActivationFunctionType
AX_X = mybir.AxisListType.X

P = 128
B, L = 8, 371
D = 128
T3 = 3
LP = T3 * P
ROWS = (P, P, L - 2 * P)
CTX, DIN = 5, 23
EPS = 1e-5
SCRATCH = 14336

L0A, L0F, L1A, L1F, L2A, L2F, L3A, L3F = range(8)

MOE = {
    L0F: dict(kind="swiglu5", routed=16, shared=1, rows=96, tiles=1, proj=2, bias=1),
    L1F: dict(kind="relu", routed=8, shared=0, rows=128, tiles=4, proj=1, bias=1),
    L2F: dict(kind="silu", routed=8, shared=0, rows=128, tiles=4, proj=2, bias=0),
    L3F: dict(kind="silu", routed=8, shared=1, rows=128, tiles=2, proj=2, bias=0),
}


class Room:

    def __init__(self, memory):
        self.memory, self.taken = memory, 0

    def lay(self, shape):
        n = 1
        for x in shape[1:]:
            n *= x
        v = self.memory[0:shape[0], self.taken:self.taken + n]
        self.taken += n
        assert self.taken <= self.memory.shape[1], self.taken
        letters = "abcdef"[:len(shape) - 1]
        if len(shape) > 2:
            v = v.rearrange("p (" + " ".join(letters) + ") -> p " + " ".join(letters),
                            **{c: x for c, x in zip(letters[1:], shape[2:])})
        return v


class Core:

    def __init__(self, nc, ctx, W, out):
        self.nc, self.ctx, self.W, self.out = nc, ctx, W, out
        self.ps = ctx.enter_context(nc.psum_tensor("psum", [P, 8, 512], F32))
        self.h = self.sb("h", [P, (B + 1) * T3, D])
        self.ident = self.sb("ident", [P, P])
        self.neghalf = self.sb("neghalf", [P, 32])
        self.ln_st = self.sb("ln_st", [P, 2, T3, 6])
        self.ln_mv = self.sb("ln_mv", [P, 2, T3, 2])
        self.ln_ve = self.sb("ln_ve", [P, 2, T3])
        self.ln_rs = self.sb("ln_rs", [P, 2, T3])
        self.xn = self.sb("xn", [P, 2, T3, D])
        self.xT = self.sb("xT", [P, 2, LP])
        self.w_l03 = self.sb("w_l03", [P, 9 * 3 * 256])
        self.w_l1 = self.sb("w_l1", [P, 8 * 1024])
        self.w_l2 = self.sb("w_l2", [P, 8 * 1536])
        self.scratch = Room(self.sb("scratch", [P, SCRATCH]))
        self.h_done = self.sem("h_done")
        self.const_ready = self.sem("const_ready")
        self.ln_var, self.ln_rstd, self.ln_norm = self.sem("ln_var"), self.sem("ln_rstd"), self.sem("ln_normed")
        self.ln_tr, self.ln_xT, self.xT_used = self.sem("ln_transposed"), self.sem("ln_xT"), self.sem("xT_used")
        self.ln_stats_done = self.sem("ln_stats")
        self.out_written = self.sem("out_written")
        self.passed = self.sem("waits_apart")
        self.phase_ended, self.phase_begun = self.sem("phase_ended"), self.sem("phase_begun")
        self.phase_sems, self.reused = None, {}
        self.loads, self.w_sem = [], {}

    def sb(self, name, shape, dt=F32):
        return self.ctx.enter_context(self.nc.sbuf_tensor(name, shape, dt))

    def sem(self, name):
        return self.ctx.enter_context(self.nc.semaphore(name))

    def phase_sem(self, name):
        sem = self.phase_sems.enter_context(self.nc.semaphore(name))
        self.reused[sem.num] = sem
        return sem

    def next_phase(self, engine, eng, number):
        eng.drain()
        if engine != "pool":
            eng.sem_inc(self.phase_ended, 1)
            eng.wait_ge(self.phase_begun, number + 1)
            return
        eng.wait_ge(self.phase_ended, 3 * (number + 1))
        for sem in self.reused.values():
            eng.sem_clear(sem)
        eng.drain()
        eng.sem_inc(self.phase_begun, 1)

    def carve(self, shape, anew=False):
        if anew:
            self.scratch.taken = 0
        return self.scratch.lay(shape)

    def tile(self, b, t, rows=P):
        return self.h[0:rows, bass.ds(b * T3 + t, 1), :]

    def load(self, key, dst, src, after=None):
        if key not in self.w_sem:
            self.w_sem[key] = [self.sem("w_" + key), 0]
        self.w_sem[key][1] += 16
        self.loads.append((key, dst, src, after))

    def weight(self, key, name, shape, broadcast=False, room=None):
        t = self.sb(name, shape)[:] if room is None else room.lay(shape)
        self.load(key, t, self.W[name].partition_broadcast(shape[0]) if broadcast else self.W[name])
        return t

    def weights_ready(self, eng, key):
        eng.wait_ge(self.w_sem[key][0], self.w_sem[key][1])

    def wait_apart(self, eng, sem, value):
        eng.wait_ge(sem, value)
        eng.sem_inc(self.passed, 1)

    def ln_stats(self, dve, pos, b, half, at=None):
        at = b if at is None else at
        n = b + 9 * pos
        for t in range(T3):
            i = dve.bn_stats(self.ln_st[:, half, t, :], self.tile(at, t).rearrange("p a d -> p (a d)"))
        i.then_inc(self.ln_stats_done, 1)
        self.wait_apart(dve, self.ln_stats_done, n * 3 + 1)
        for t in range(T3):
            i = dve.bn_aggr(self.ln_mv[:, half, t, :], self.ln_st[:, half, t, :])
        i.then_inc(self.ln_stats_done, 1)
        dve.wait_ge(self.ln_stats_done, n * 3 + 2)
        dve.tensor_scalar(self.ln_ve[:, half, :], self.ln_mv[:, half, :, 1], EPS, None, ALU.add).then_inc(self.ln_var, 1)

    def ln_power(self, pool, pos, b, half):
        pool.wait_ge(self.ln_var, b + 9 * pos + 1)
        pool.tensor_tensor(self.ln_rs[:, half, :], self.ln_ve[:, half, :], self.neghalf[:, 0:T3],
                           ALU.pow).then_inc(self.ln_rstd, 1)

    def ln_apply(self, dve, pos, b, half, at=None):
        n, at = b + 9 * pos, b if at is None else at
        dve.wait_ge(self.ln_rstd, n + 1)
        for t in range(T3):
            i = dve.tensor_scalar(self.xn[:, half, t, :], self.tile(at, t).rearrange("p a d -> p (a d)"),
                                  self.ln_mv[:, half, t, 0:1], self.ln_rs[:, half, t:t + 1], ALU.subtract, ALU.mult)
        i.then_inc(self.ln_norm, 1)
        dve.sem_inc(self.ln_stats_done, 1)

    def ln_transpose(self, pe, pos, b, half, bank=7):
        n = b + 9 * pos
        pe.wait_ge(self.ln_norm, n + 1)
        pe.wait_ge(self.ln_xT, n)
        for t in range(T3):
            i = pe.transpose(self.ps[:, bank, t * P:(t + 1) * P], self.xn[:, half, t, :], self.ident[:])
        i.then_inc(self.ln_tr, 1)

    def ln_copy(self, act, pos, b, half, used, bank=7):
        act.wait_ge(self.ln_tr, b + 9 * pos + 1)
        act.wait_ge(self.xT_used, used)
        act.copy(self.xT[:, half, :], self.ps[:, bank, 0:LP]).then_inc(self.ln_xT, 1)


def tdnn(k, key="tok"):
    ps, sem = k.ps, k.phase_sem
    w = k.weight(key, "tok_w", [CTX * DIN, D])
    cols = k.weight(key, "tok_cols", [D, 3])
    patches = k.carve([CTX * DIN, B, L], anew=True)
    y = k.carve([P, B, L])
    yn = k.carve([P, 2, LP])
    stats, bn = k.carve([P, B, 6]), k.carve([P, 8])
    patched, product, relued = sem("tok_patches"), sem("tok_product"), sem("tok_relu")
    st, steps, rstd = sem("tok_stats"), sem("tok_bn_steps"), sem("tok_rstd")
    normed, turned, zeroed = sem("tok_normed"), sem("tok_transposed"), sem("tok_zeroed")

    def sync(sp):
        for c in range(CTX):
            sp.dma_start(patches[c * DIN:(c + 1) * DIN], k.W["x"][:, :, c:c + L]).then_inc(patched, 16)

    def pe(eng):
        eng.wait_ge(patched, 16 * CTX)
        k.weights_ready(eng, key)
        with eng.Fori(0, B // 2) as i:
            for half in range(2):
                eng.wait_ge(relued, i * 2)
                eng.matmul(ps[:, half, 0:L], w[:], patches[:, i * 2 + half, :], start=True, stop=True).then_inc(product, 1)
        eng.wait_ge(k.const_ready, 2)
        with eng.Fori(0, B // 2) as i:
            for half in range(2):
                eng.wait_ge(normed, i * 2 + half + 1)
                eng.wait_ge(k.h_done, i * 2)
                for t in range(T3):
                    m = eng.transpose(ps[:, 2 + half, t * P:(t + 1) * P], yn[:, half, t * P:(t + 1) * P], k.ident[:])
                m.then_inc(turned, 1)

    def act(eng):
        k.weights_ready(eng, key)
        with eng.Fori(0, B // 2) as i:
            for half in range(2):
                eng.wait_ge(product, i * 2 + half + 1)
                eng.activation(y[:, i * 2 + half, :], ps[:, half, 0:L], ACT.Relu, bias=cols[:, 0:1]).then_inc(relued, 1)
        eng.wait_ge(relued, B)
        eng.wait_ge(steps, 5)
        eng.wait_ge(zeroed, 1)
        with eng.Fori(0, B // 2) as i:
            for half in range(2):
                eng.wait_ge(turned, i * 2)
                eng.activation(yn[:, half, 0:L], y[:, i * 2 + half, :], ACT.Identity,
                               bias=bn[:, 4:5], scale=bn[:, 3:4]).then_inc(normed, 1)

    def dve(eng):
        eng.memset(yn, 0.0).then_inc(zeroed, 1)
        eng.memset(k.h[:], 0.0).then_inc(zeroed, 1)
        with eng.Fori(0, B // 2) as i:
            for half in range(2):
                eng.wait_ge(relued, i * 2 + half + 1)
                eng.bn_stats(stats[:, i * 2 + half, :], y[:, i * 2 + half, :]).then_inc(st, 1)
        eng.wait_ge(st, B)
        eng.bn_aggr(bn[:, 0:2], stats.rearrange("p a b -> p (a b)")).then_inc(steps, 1)
        eng.wait_ge(steps, 1)
        eng.tensor_scalar(bn[:, 2:3], bn[:, 1:2], EPS, None, ALU.add).then_inc(steps, 1)
        eng.wait_ge(rstd, 1)
        k.weights_ready(eng, key)
        eng.tensor_tensor(bn[:, 3:4], bn[:, 5:6], cols[:, 1:2], ALU.mult).then_inc(steps, 1)
        eng.wait_ge(steps, 3)
        eng.tensor_tensor(bn[:, 6:7], bn[:, 0:1], bn[:, 3:4], ALU.mult).then_inc(steps, 1)
        eng.wait_ge(steps, 4)
        eng.tensor_tensor(bn[:, 4:5], cols[:, 2:3], bn[:, 6:7], ALU.subtract).then_inc(steps, 1)
        eng.wait_ge(zeroed, 2)
        with eng.Fori(0, B // 2) as i:
            for half in range(2):
                eng.wait_ge(turned, i * 2 + half + 1)
                eng.tensor_copy(k.h[:, bass.ds((i * 2 + half) * T3, T3), :],
                                ps[:, 2 + half, 0:LP].rearrange("p (t d) -> p t d", t=T3)).then_inc(k.h_done, 1)

    def pool(eng):
        eng.wait_ge(steps, 2)
        eng.wait_ge(k.const_ready, 2)
        eng.tensor_tensor(bn[:, 5:6], bn[:, 2:3], k.neghalf[:, 0:1], ALU.pow).then_inc(rstd, 1)

    return dict(sync=sync, pe=pe, act=act, dve=dve, pool=pool)


def experts(k, pos, layer):
    ps, sem = k.ps, k.sem
    g = MOE[layer]
    kind, E, R, FT, PJ, bias = g["kind"], g["routed"], g["rows"], g["tiles"], g["proj"], g["bias"]
    N = E + g["shared"]
    F = R * FT
    O = N + bias
    key = f"l{layer // 2}f"
    big = {L0F: k.w_l03, L1F: k.w_l1, L2F: k.w_l2, L3F: k.w_l03}[layer]
    w1 = big[:, 0:N * PJ * F].rearrange("p (e k f) -> p e k f", e=N, k=PJ)
    w2 = big[0:R, N * PJ * F:N * PJ * F + N * FT * D].rearrange("p (e f d) -> p e f d", e=N, f=FT)
    gate = k.weight(key, key + "_gate", [D, E])
    gate_b = None if layer == L2F else k.weight(key, key + "_gate_b", [P, T3 * E], broadcast=True)
    b1 = None if kind == "silu" else k.weight(key, key + "_b1", [R, N * FT * PJ])
    b2 = k.weight(key, key + "_b2", [N, D]) if bias else None
    scal = k.weight(key, key + "_scal", [P, N * 5], broadcast=True) if kind == "swiglu5" else None
    after = None
    if layer == L3F and pos >= 6:
        after = 2
    if layer in (L1F, L2F) and pos >= 3:
        after = 1
    k.load(key, w1, k.W[key + "_w1"], after)
    k.load(key, w2, k.W[key + "_w2"], after)
    hid = k.carve([R, 2, FT, LP], anew=True)
    acc = k.carve([P, 2, T3, D])
    lg, mx, ix = k.carve([P, T3, E]), k.carve([P, T3, 8]), k.carve([P, T3, 8]).bitcast(U32)
    ixf, ex, wk = k.carve([P, T3, 2]), k.carve([P, T3, 2]), k.carve([P, T3, 4])
    oh, iota = k.carve([P, 2, T3, E]), k.carve([P, T3, E])
    cw = k.carve([P, 2, T3, N])
    if kind == "silu":
        gated = k.carve([R, 2, LP])
    if layer == L3F:
        sc, ms = k.carve([P, T3, E]), k.carve([P, T3, 8])
    if bias:
        cwT = k.carve([N, 2, LP])
    if kind == "swiglu5":
        gb, ub = k.carve([R, 2, LP]), k.carve([R, 2, LP])
        gc, uc, th, sg = k.carve([R, 2, LP]), k.carve([R, 2, LP]), k.carve([R, LP]), k.carve([R, 2, LP])
        up_b = k.carve([R, N])
        lim = k.carve([P, 6, N, 2])
        half_alpha, half_scale = k.carve([P, N]), k.carve([P, N])
        cws = k.carve([P, 2, T3, N])
    s = lambda name: k.phase_sem(f"{key}_{name}")
    hidden, ready = s("hidden"), s("hid_ready")
    y, added = s("y"), s("y_added")
    logits, exp_in, exp = s("logits"), s("exp_in"), s("exp")
    routed, cw_turned, cwT_ready = s("routed"), s("cw_transposed"), s("cwT_ready")
    steps, set_up = s("routing_steps"), s("set_up")
    if kind == "silu":
        gate_half = s("silu_gate")
    if kind == "swiglu5":
        biased, clipped, tanhed, glued, limits = s("biased"), s("clipped"), s("tanh"), s("gate_times_sigmoid"), s("limits")
    SLOTS = 4 // PJ
    last = N - 1
    LAG = 2 if kind == "swiglu5" else 1
    TURN, LOGITS, ROUTE = 2, 3, 5
    RS = {L0F: 10, L1F: 9, L2F: 9, L3F: 11}[layer]

    def hid_bank(half, e, f, p):
        return 1 + ((half * N + e) * FT + f) % SLOTS * PJ + p

    vacated, VAC = (biased, 2) if kind == "swiglu5" else (ready, 1)
    READY0 = 1 if kind == "swiglu5" else SLOTS

    def hid_free(i, half, e):
        return i * (2 * O) + half * O + e + (bias if e >= 2 else 0)

    def pe(eng):
        def route_logits(b, half):
            eng.wait_ge(k.ln_xT, b + 9 * pos + 1)
            eng.wait_ge(routed, b)
            for t in range(T3):
                m = eng.matmul(ps[:, 0, t * E:(t + 1) * E], k.xT[:, half, t * P:(t + 1) * P], gate[:], start=True, stop=True)
            m.then_inc(logits, 1)

        def turn_cw(b, half):
            eng.wait_ge(routed, b + 1)
            for t in range(T3):
                m = eng.transpose(ps[0:N, 0, t * P:(t + 1) * P], cw[:, half, t, :], k.ident[:])
            m.then_inc(cw_turned, 1)

        def project(i, half, e):
            for f in range(FT):
                c = (half * N + e) * FT + f
                eng.wait_ge(vacated, (i * (2 * N * FT) + c + 1) * VAC)
                for p in range(PJ):
                    m = eng.matmul(ps[0:R, hid_bank(half, e, f, p), 0:L], w1[:, e, p, f * R:(f + 1) * R],
                                   k.xT[:, half, 0:L], start=True, stop=True)
                m.then_inc(hidden, 1)

        def output(i, half, o):
            e, n = o - bias, half * O + o
            eng.wait_ge(added, i * (2 * O) + n)
            if e < 0:
                eng.wait_ge(cwT_ready, i * 2 + half + 1)
                for t in range(T3):
                    m = eng.matmul(ps[0:ROWS[t], 5 + n % 2, t * D:(t + 1) * D], cwT[:, half, t * P:t * P + ROWS[t]],
                                   b2[:], start=True, stop=True)
            else:
                eng.wait_ge(ready, i * (2 * N * FT) + (half * N + e + 1) * FT + READY0)
                for t in range(T3):
                    for f in range(FT):
                        m = eng.matmul(ps[0:ROWS[t], 5 + n % 2, t * D:(t + 1) * D],
                                       hid[:, (half * N + e) % 2, f, t * P:t * P + ROWS[t]], w2[:, e, f, :],
                                       start=(f == 0), stop=(f == FT - 1))
                        if e == last and t == 0 and f == 0:
                            m.then_inc(k.xT_used, 1)
            m.then_inc(y, 1)

        k.weights_ready(eng, key)
        eng.wait_ge(k.h_done, 8 * (pos + 1))
        eng.sem_inc(y, 1)
        k.ln_transpose(eng, pos, 0, 0)
        route_logits(0, 0)
        if bias:
            turn_cw(0, 0)
        with eng.Fori(0, B // 2) as i:
            for half in range(2):
                nb = i * 2 + half + 1
                for e in range(N):
                    project(i, half, e)
                    if e == 1 and bias:
                        output(i, half, 0)
                    if e >= LAG:
                        output(i, half, e - LAG + bias)
                    if e == TURN:
                        k.ln_transpose(eng, pos, nb, 1 - half)
                    if e == LOGITS:
                        route_logits(nb, 1 - half)
                    if e == last and bias:
                        turn_cw(nb, 1 - half)
                for o in range(O - LAG, O):
                    output(i, half, o)

    def act(eng):
        def exponent(b):
            eng.wait_ge(exp_in, b + 1)
            n = 2 if layer == L3F else 1
            eng.activation(ex[:, :, 0:n], wk[:, :, 0:n], ACT.Exp, scale=-1.0 if layer == L3F else 1.0).then_inc(exp, 1)

        def copy_cwT(b, half):
            eng.wait_ge(cw_turned, b + 1)
            eng.copy(cwT[:, half, :], ps[0:N, 0, 0:LP]).then_inc(cwT_ready, 1)

        k.weights_ready(eng, key)
        eng.wait_ge(k.h_done, 8 * (pos + 1))
        k.ln_copy(eng, pos, 0, 0, 8 * pos)
        if kind != "silu":
            eng.sem_inc(vacated, SLOTS * VAC)
        if kind == "swiglu5":
            eng.wait_ge(limits, 1)
            eng.activation(lim[:, 1], lim[:, 0], ACT.Abs).then_inc(limits, 1)
            eng.wait_ge(limits, 2)
            eng.activation(lim[:, 2], lim[:, 1], ACT.Exp, scale=-1.0).then_inc(limits, 1)
            eng.wait_ge(limits, 3)
            eng.activation(lim[:, 3], lim[:, 2], ACT.Ln, bias=1.0).then_inc(limits, 1)
            eng.wait_ge(limits, 8)
        exponent(0)
        if bias:
            copy_cwT(0, 0)
        with eng.Fori(0, B // 2) as i:
            for half in range(2):
                nb = i * 2 + half + 1

                def tanh(e):
                    c = i * (2 * N) + half * N + e
                    eng.wait_ge(clipped, c * 2 + 3)
                    eng.wait_ge(glued, c)
                    eng.activation(th[:, 0:L], gc[:, (half * N + e) % 2, 0:L], ACT.Tanh, scale=half_alpha[0:R, e:e + 1]).then_inc(tanhed, 1)

                for e in range(N):
                    turn = half * N + e
                    for f in range(FT):
                        c = i * (2 * N * FT) + turn * FT + f
                        eng.wait_ge(hidden, c + 1)
                        if kind == "relu":
                            if f == 0:
                                eng.wait_ge(y, hid_free(i, half, e))
                            eng.activation(hid[:, turn % 2, f, 0:L], ps[0:R, hid_bank(half, e, f, 0), 0:L], ACT.Relu,
                                           bias=b1[:, e * FT + f:e * FT + f + 1]).then_inc(ready, 1)
                        elif kind == "silu":
                            eng.wait_ge(ready, c + 1)
                            eng.activation(gated[:, (turn * FT + f) % 2, 0:L], ps[0:R, hid_bank(half, e, f, 0), 0:L],
                                           ACT.Silu).then_inc(gate_half, 1)
                        else:
                            eng.wait_ge(clipped, c * 2)
                            eng.activation(gb[:, turn % 2, 0:L], ps[0:R, hid_bank(half, e, 0, 0), 0:L], ACT.Identity,
                                           bias=b1[:, 2 * e:2 * e + 1]).then_inc(biased, 1)
                            eng.activation(ub[:, turn % 2, 0:L], ps[0:R, hid_bank(half, e, 0, 1), 0:L], ACT.Identity,
                                           bias=up_b[:, e:e + 1]).then_inc(biased, 1)
                            tanh(e)
                    if e == TURN:
                        k.ln_copy(eng, pos, nb, 1 - half, nb - 1 + 8 * pos)
                    if e == ROUTE:
                        exponent(nb)
                    if e == last and bias:
                        copy_cwT(nb, 1 - half)

    def dve(eng):
        sh = [P, T3, E]

        def step(ins, n, b):
            ins.then_inc(steps, 1)
            if n <= 2:
                k.wait_apart(eng, steps, b * RS + n)
            else:
                eng.wait_ge(steps, b * RS + n)

        def largest(b):
            eng.wait_ge(logits, b + 1)
            lgp = ps[:, 0, 0:T3 * E].rearrange("p (t e) -> p t e", t=T3)
            if layer == L3F:
                eng.tensor_copy(sc, lgp)
            if layer == L2F:
                step(eng.tensor_copy(lg, lgp), 1, b)
            else:
                step(eng.tensor_tensor(lg, lgp, gate_b.rearrange("p (t e) -> p t e", t=T3), ALU.add), 1, b)
            for t in range(T3):
                m = eng.max(mx[:, t, :], lg[:, t, :])
                if layer == L3F:
                    m = eng.max(ms[:, t, :], sc[:, t, :])
            step(m, 2, b)
            for t in range(T3):
                m = eng.max_index(ix[:, t, :], mx[:, t, :], lg[:, t, :])
            step(m, 3, b)
            if layer == L3F:
                eng.tensor_copy(wk[:, :, 0:2], ms[:, :, 0:2]).then_inc(exp_in, 1)
            else:
                eng.tensor_tensor(wk[:, :, 0:1], mx[:, :, 1:2], mx[:, :, 0:1], ALU.subtract).then_inc(exp_in, 1)

        def weigh(b, half):
            eng.tensor_copy(ixf, ix[:, :, 0:2])
            eng.wait_ge(exp, b + 1)
            if layer == L3F:
                step(eng.tensor_scalar(wk[:, :, 2:4], ex, 1.0, None, ALU.add), 4, b)
                step(eng.reciprocal(wk[:, :, 0:2], wk[:, :, 2:4]), 5, b)
                step(eng.tensor_tensor(wk[:, :, 2:3], wk[:, :, 0:1], wk[:, :, 1:2], ALU.add), 6, b)
                step(eng.reciprocal(wk[:, :, 3:4], wk[:, :, 2:3]), 7, b)
                step(eng.tensor_tensor(ex, wk[:, :, 0:2], wk[:, :, 3:4].to_broadcast([P, T3, 2]), ALU.mult), 8, b)
                wa, wb, n = ex[:, :, 0:1], ex[:, :, 1:2], 9
            else:
                step(eng.tensor_scalar(wk[:, :, 1:2], ex[:, :, 0:1], 1.0, None, ALU.add), 4, b)
                step(eng.reciprocal(wk[:, :, 2:3], wk[:, :, 1:2]), 5, b)
                step(eng.tensor_tensor(wk[:, :, 3:4], wk[:, :, 2:3], ex[:, :, 0:1], ALU.mult), 6, b)
                wa, wb, n = wk[:, :, 2:3], wk[:, :, 3:4], 7
            eng.tensor_tensor(oh[:, 0], iota, ixf[:, :, 0:1].to_broadcast(sh), ALU.is_equal)
            step(eng.tensor_tensor(oh[:, 1], iota, ixf[:, :, 1:2].to_broadcast(sh), ALU.is_equal), n, b)
            eng.tensor_tensor(oh[:, 0], oh[:, 0], wa.to_broadcast(sh), ALU.mult)
            step(eng.tensor_tensor(oh[:, 1], oh[:, 1], wb.to_broadcast(sh), ALU.mult), n + 1, b)
            if bias:
                eng.wait_ge(cw_turned, b)
            step(eng.tensor_tensor(cw[:, half, :, 0:E], oh[:, 0], oh[:, 1], ALU.add), n + 2, b)
            if kind == "swiglu5":
                step(eng.tensor_tensor(cws[:, half], cw[:, half], half_scale.unsqueeze(1).to_broadcast([P, T3, N]),
                                       ALU.mult), n + 3, b)
            eng.sem_inc(routed, 1)

        def clip(e, c, half, p):
            eng.wait_ge(biased, (c + SLOTS) * 2 + 1 + p)
            src, dst = ((gb, gc), (ub, uc))[p]
            eng.tensor_scalar(dst[:, (half * N + e) % 2, 0:L], src[:, (half * N + e) % 2, 0:L], lim[0:R, 5, e, p:p + 1],
                              lim[0:R, 4, e, p:p + 1], ALU.max, ALU.min).then_inc(clipped, 1)

        def add(i, half, o):
            e, n, b = o - bias, half * O + o, i * 2 + half
            eng.wait_ge(y, i * (2 * O) + n + 2)
            eng.wait_ge(added, i * (2 * O) + n + 1)
            for t in range(T3):
                r = ROWS[t]
                if e < 0 or (e >= E and kind != "swiglu5"):
                    w = 1.0
                else:
                    w = (cws if kind == "swiglu5" else cw)[0:r, half, t, e:e + 1]
                src = k.tile(b, t, r) if o == 0 else acc[0:r, half, t:t + 1, :]
                dst = k.tile(b, t, r) if o == O - 1 else acc[0:r, half, t:t + 1, :]
                m = eng.scalar_tensor_tensor(dst, ps[0:r, 5 + n % 2, t * D:(t + 1) * D].unsqueeze(1), w, src, ALU.mult, ALU.add)
            m.then_inc(added, 1)
            if o == O - 1:
                eng.wait_ge(added, i * (2 * O) + n + 2)
                eng.sem_inc(k.h_done, 1)

        eng.wait_ge(k.h_done, 8 * (pos + 1))
        k.weights_ready(eng, key)
        k.ln_stats(eng, pos, 0, 0)
        k.ln_apply(eng, pos, 0, 0)
        eng.sem_inc(added, 1)
        if kind == "silu":
            eng.sem_inc(vacated, SLOTS)
        if N > E:
            eng.memset(cw, 1.0).then_inc(set_up, 1)
        if kind == "swiglu5":
            s5 = scal.rearrange("p (e c) -> p e c", c=5)
            eng.tensor_copy(lim[:, 0], s5[:, :, 3:5]).then_inc(limits, 1)
            eng.tensor_scalar(half_alpha, s5[:, :, 0], 0.5, None, ALU.mult)
            eng.tensor_scalar(half_scale, s5[:, :, 1], 0.5, None, ALU.mult)
            eng.wait_ge(limits, 4)
            eng.tensor_scalar(lim[:, 1], lim[:, 0], 0.0, None, ALU.max).then_inc(limits, 1)
            eng.wait_ge(limits, 5)
            eng.tensor_tensor(lim[:, 4], lim[:, 1], lim[:, 3], ALU.add).then_inc(limits, 1)
            eng.wait_ge(limits, 6)
            eng.tensor_scalar(lim[:, 5], lim[:, 4], -1.0, None, ALU.mult).then_inc(limits, 1)
            eng.wait_ge(limits, 7)
            for j in (4, 5):
                eng.tensor_tensor(lim[:, j, :, 1], lim[:, j, :, 1], s5[:, :, 2], ALU.add)
            eng.tensor_tensor(up_b, b1[:].rearrange("p (e c) -> p e c", c=2)[:, :, 1], s5[0:R, :, 2], ALU.add).then_inc(limits, 1)
            eng.wait_ge(limits, 8)
            eng.sem_inc(ready, READY0)
            eng.sem_inc(clipped, 2)
        eng.wait_ge(set_up, 1 + (N > E))
        largest(0)
        weigh(0, 0)
        with eng.Fori(0, B // 2) as i:
            for half in range(2):
                nb = i * 2 + half + 1
                k.ln_stats(eng, pos, nb, 1 - half)
                for e in range(N):
                    turn = half * N + e
                    for f in range(FT):
                        c = i * (2 * N * FT) + turn * FT + f
                        if kind == "silu":
                            eng.wait_ge(gate_half, c + 1)
                            if f == 0:
                                eng.wait_ge(y, hid_free(i, half, e))
                            eng.tensor_tensor(hid[:, turn % 2, f, 0:L], gated[:, (turn * FT + f) % 2, 0:L],
                                              ps[0:R, hid_bank(half, e, f, 1), 0:L], ALU.mult).then_inc(ready, 1)
                        elif kind == "swiglu5":
                            eng.wait_ge(ready, c)
                            clip(e, c, half, 0)
                            clip(e, c, half, 1)
                            if e >= 2:
                                add(i, half, e - 2)
                            eng.wait_ge(tanhed, c + 1)
                            eng.scalar_tensor_tensor(sg[:, turn % 2, 0:L], th[:, 0:L], 1.0, gc[:, turn % 2, 0:L], ALU.add, ALU.mult).then_inc(glued, 1)
                    if e >= 1 and kind != "swiglu5":
                        for o in range(e - 1 + bias if e > 1 else 0, e + bias):
                            add(i, half, o)
                    if e == 0:
                        k.ln_apply(eng, pos, nb, 1 - half)
                    if e == LOGITS:
                        largest(nb)
                    if e == ROUTE:
                        weigh(nb, 1 - half)
                for o in range(O - (3 if kind == "swiglu5" else 1), O):
                    add(i, half, o)

    def pool(eng):
        eng.wait_ge(k.h_done, 8 * (pos + 1))
        eng.iota(iota, [[0, T3], [1, E]], base=0, channel_multiplier=0, allow_small_or_imprecise_dtypes=True).then_inc(set_up, 1)
        k.ln_power(eng, pos, 0, 0)
        with eng.Fori(0, B // 2) as i:
            for half in range(2):
                k.ln_power(eng, pos, i * 2 + half + 1, 1 - half)
                for e in range(N if kind == "swiglu5" else 0):
                    turn = half * N + e
                    c = i * (2 * N) + turn
                    eng.wait_ge(glued, c + 1)
                    eng.wait_ge(clipped, c * 2 + 4)
                    eng.wait_ge(y, hid_free(i, half, e))
                    eng.tensor_tensor(hid[:, turn % 2, 0, 0:L], uc[:, turn % 2, 0:L], sg[:, turn % 2, 0:L], ALU.mult).then_inc(ready, 1)

    return dict(pe=pe, act=act, dve=dve, pool=pool)


def linear_attention(k, pos, layer):
    ps, key = k.ps, "l3a"
    w = k.weight(key, key + "_w", [P, 4 * D])
    bn = k.weight(key, key + "_bn", [P, 5 * 4])
    heads = k.weight(key, key + "_heads", [P, D])
    xs = k.carve([P, 3, LP], anew=True)
    kv = k.carve([P, 2, T3, D])
    mixed, o, proj = k.carve([P, D]), k.carve([P, LP]), k.carve([P, LP])
    ve, rs, scale, cols = k.carve([P, 4]), k.carve([P, 4]), k.carve([P, 4]), k.carve([P, 3, 4])
    s = lambda name: k.phase_sem(f"{key}_{name}")
    projected, relued, turned, copied = s("projected"), s("relued"), s("kv_turned"), s("kv_copied")
    kv_done, masked, mixed_q, mixed_relu = s("kv"), s("kv_masked"), s("mixed"), s("mixed_relu")
    last, last_relu, back, set_up, rstd = s("p"), s("p_relu"), s("p_turned"), s("set_up"), s("rstd")

    def pe(eng):
        def batch(b, half):
            eng.wait_ge(k.ln_xT, b + 9 * pos + 1)
            eng.wait_ge(k.h_done, b + 8 * (pos + 1))
            for j in range(3):
                eng.matmul(ps[:, j, 0:L], w[:, j * D:(j + 1) * D], k.xT[:, half, 0:L], start=True, stop=True).then_inc(projected, 1)
            for j in range(2):
                eng.wait_ge(relued, 3 * b + 2 + j)
                for t in range(T3):
                    m = eng.transpose(ps[0:ROWS[t], 3 + j, t * D:(t + 1) * D], xs[:, 1 + j, t * P:t * P + ROWS[t]], k.ident[:])
                    if j == 0 and t == 0:
                        m.then_inc(k.xT_used, 1)
                m.then_inc(turned, 1)
            k.ln_transpose(eng, pos, b + 1, 1 - half)
            eng.wait_ge(copied, 2 * b + 2)
            for t in range(T3):
                m = eng.matmul(ps[:, 5, 0:D], kv[0:ROWS[t], 0, t, :], kv[0:ROWS[t], 1, t, :], start=(t == 0), stop=(t == T3 - 1))
            m.then_inc(kv_done, 1)
            eng.wait_ge(masked, b + 1)
            eng.matmul(ps[:, 6, 0:L], mixed, xs[:, 0, 0:L], start=True, stop=True).then_inc(mixed_q, 1)
            eng.wait_ge(mixed_relu, b + 1)
            eng.matmul(ps[:, 0, 0:L], w[:, 3 * D:4 * D], o[:, 0:L], start=True, stop=True).then_inc(last, 1)
            eng.wait_ge(last_relu, b + 1)
            for t in range(T3):
                m = eng.transpose(ps[0:ROWS[t], 1, t * D:(t + 1) * D], proj[:, t * P:t * P + ROWS[t]], k.ident[:])
            m.then_inc(back, 1)

        k.weights_ready(eng, key)
        eng.wait_ge(k.h_done, 8 * (pos + 1))
        k.ln_transpose(eng, pos, 0, 0)
        with eng.Fori(0, B // 2) as i:
            for half in range(2):
                batch(i * 2 + half, half)

    def act(eng):
        def relu(dst, src, j):
            return eng.activation(dst, src, ACT.Relu, bias=cols[:, 2, j:j + 1], scale=scale[:, j:j + 1])

        def batch(b, half):
            for j in range(3):
                eng.wait_ge(projected, 3 * b + 1 + j)
                eng.wait_ge(mixed_q, b)
                relu(xs[:, j, 0:L], ps[:, j, 0:L], j).then_inc(relued, 1)
            k.ln_copy(eng, pos, b + 1, 1 - half, b + 8 * pos)
            eng.wait_ge(mixed_q, b + 1)
            eng.activation(o[:, 0:L], ps[:, 6, 0:L], ACT.Relu).then_inc(mixed_relu, 1)
            eng.wait_ge(last, b + 1)
            relu(proj[:, 0:L], ps[:, 0, 0:L], 3).then_inc(last_relu, 1)

        eng.wait_ge(k.h_done, 8 * (pos + 1))
        k.ln_copy(eng, pos, 0, 0, 8 * pos)
        eng.wait_ge(set_up, 5)
        with eng.Fori(0, B // 2) as i:
            for half in range(2):
                batch(i * 2 + half, half)

    def dve(eng):
        def batch(b, half):
            k.ln_stats(eng, pos, b + 1, 1 - half)
            for j in range(2):
                eng.wait_ge(turned, 2 * b + 1 + j)
                eng.wait_ge(kv_done, b)
                eng.tensor_copy(kv[:, j, 0:2, :], ps[:, 3 + j, 0:2 * D].rearrange("p (t d) -> p t d", t=2))
                eng.tensor_copy(kv[0:ROWS[2], j, 2, :], ps[0:ROWS[2], 3 + j, 2 * D:3 * D]).then_inc(copied, 1)
            k.ln_apply(eng, pos, b + 1, 1 - half)
            eng.wait_ge(kv_done, b + 1)
            eng.scalar_tensor_tensor(mixed, ps[:, 5, 0:D], 0.125, heads[:], ALU.mult, ALU.mult).then_inc(masked, 1)
            eng.wait_ge(back, b + 1)
            for t in range(T3):
                r = ROWS[t]
                m = eng.tensor_tensor(k.tile(b, t, r), k.tile(b, t, r), ps[0:r, 1, t * D:(t + 1) * D].unsqueeze(1), ALU.add)
            m.then_inc(k.h_done, 1)

        eng.wait_ge(k.h_done, 8 * (pos + 1))
        k.ln_stats(eng, pos, 0, 0)
        k.ln_apply(eng, pos, 0, 0)
        k.weights_ready(eng, key)
        c = lambda n: bn[:, 4 * n:4 * n + 4]
        eng.tensor_scalar(ve, c(4), EPS, None, ALU.add).then_inc(set_up, 1)
        eng.tensor_tensor(cols[:, 0], c(0), c(3), ALU.subtract).then_inc(set_up, 1)
        eng.wait_ge(rstd, 1)
        eng.tensor_tensor(scale, rs, c(1), ALU.mult).then_inc(set_up, 1)
        eng.wait_ge(set_up, 3)
        eng.tensor_tensor(cols[:, 1], cols[:, 0], scale, ALU.mult).then_inc(set_up, 1)
        eng.wait_ge(set_up, 4)
        eng.tensor_tensor(cols[:, 2], cols[:, 1], c(2), ALU.add).then_inc(set_up, 1)
        with eng.Fori(0, B // 2) as i:
            for half in range(2):
                batch(i * 2 + half, half)

    def pool(eng):
        eng.wait_ge(k.h_done, 8 * (pos + 1))
        k.ln_power(eng, pos, 0, 0)
        eng.wait_ge(set_up, 1)
        eng.tensor_tensor(rs, ve, k.neghalf[:, 0:4], ALU.pow).then_inc(rstd, 1)
        with eng.Fori(0, B // 2) as i:
            for half in range(2):
                k.ln_power(eng, pos, i * 2 + half + 1, 1 - half)

    return dict(pe=pe, act=act, dve=dve, pool=pool)


def window_attention(k, pos, layer):
    ps, key = k.ps, "l1a"
    w = k.weight(key, key + "_w", [P, 3 * D])
    out_b = k.weight(key, key + "_out_b", [P, D], broadcast=True)
    qT, kT = k.carve([P, LP], anew=True), k.carve([P, P + LP])
    vo, probs, pT = k.carve([P, T3, D]), k.carve([P, T3, 2 * P]), k.carve([P, 5, P])
    mx, bias, sums, inv = k.carve([P, T3]), k.carve([P, T3]), k.carve([P, T3]), k.carve([P, T3])
    hb = k.carve([P, 2, T3, D])
    mask, ident = k.carve([P, 64]).bitcast(BF16), k.carve([P, 64]).bitcast(BF16)
    scale = float(D) ** -0.5
    s = lambda name: k.phase_sem(f"{key}_{name}")
    set_up, projected, copied, vproj, vcopied = s("set_up"), s("qk"), s("qk_copied"), s("values"), s("values_copied")
    scored, maxed, exped, turned, turned_copied = s("scores"), s("max"), s("exp"), s("probs_turned"), s("probs_copied")
    inverted, mixed, biased = s("sums_inverted"), s("mixed"), s("h_biased")
    PLACES = [(0, 0, 1, 0), (1, 0, 2, 0), (2, 1, 0, 1), (3, 1, 1, 1), (4, 1, 2, 1)]

    def pe(eng):
        def batch(b, half):
            eng.wait_ge(k.ln_xT, b + 9 * pos + 1)
            eng.wait_ge(turned_copied, 2 * b)
            for j in range(2):
                eng.matmul(ps[:, j, 0:LP], w[:, j * D:(j + 1) * D], k.xT[:, half, :], start=True, stop=True).then_inc(projected, 1)
            eng.wait_ge(copied, 2 * b + 2)
            for t in range(T3):
                m = eng.matmul(ps[:, 3 + t, 0:2 * P], qT[:, t * P:(t + 1) * P], kT[:, t * P:(t + 2) * P], start=True, stop=False)
                if t == 0:
                    m.then_inc(k.xT_used, 1)
                m = eng.matmul(ps[:, 3 + t, P:2 * P], ident, mask, start=False, stop=True)
            m.then_inc(scored, 1)
            for t in range(T3):
                m = eng.matmul(ps[:, 2, t * D:(t + 1) * D], kT[:, (t + 1) * P:(t + 2) * P], w[:, 2 * D:3 * D], start=True, stop=True)
            m.then_inc(vproj, 1)
            k.ln_transpose(eng, pos, b + 1, 1 - half)
            for n, bank, t, side in PLACES:
                eng.wait_ge(exped, 3 * b + 1 + t)
                m = eng.transpose(ps[:, bank, n % 2 * P if bank == 0 else t * P:(n % 2 if bank == 0 else t) * P + P],
                                  probs[:, t, side * P:(side + 1) * P], k.ident[:])
                if n in (1, 4):
                    m.then_inc(turned, 1)
            eng.wait_ge(turned_copied, 2 * b + 2)
            eng.wait_ge(vcopied, b + 1)
            eng.wait_ge(k.h_done, b + 8 * (pos + 1))
            for t in range(T3):
                r = ROWS[t]
                if t > 0:
                    eng.matmul(ps[0:r, 6, t * D:(t + 1) * D], pT[:, t - 1, 0:r], vo[:, t - 1, :], start=True, stop=False)
                m = eng.matmul(ps[0:r, 6, t * D:(t + 1) * D], pT[:, 2 + t, 0:r], vo[:, t, :], start=(t == 0), stop=True)
            m.then_inc(mixed, 1)

        k.weights_ready(eng, key)
        eng.wait_ge(k.h_done, 8 * (pos + 1))
        k.ln_transpose(eng, pos, 0, 0)
        eng.wait_ge(set_up, 3)
        with eng.Fori(0, B // 2) as i:
            for half in range(2):
                batch(i * 2 + half, half)

    def act(eng):
        def batch(b, half):
            eng.wait_ge(projected, 2 * b + 1)
            eng.wait_ge(scored, b)
            eng.copy(qT, ps[:, 0, 0:LP]).then_inc(copied, 1)
            for t in range(T3):
                if t == 0:
                    eng.wait_ge(maxed, 2 * b + 2)
                    eng.wait_ge(turned, 2 * b)
                    eng.wait_ge(inverted, b)
                eng.activation(probs[:, t, :], ps[:, 3 + t, 0:2 * P], ACT.Exp, bias=bias[:, t:t + 1], scale=scale,
                               accum_out=sums[:, t:t + 1]).then_inc(exped, 1)
            k.ln_copy(eng, pos, b + 1, 1 - half, b + 8 * pos)
            eng.wait_ge(turned, 2 * b + 2)
            eng.wait_ge(mixed, b)
            eng.copy(pT[:, 2:5, :], ps[:, 1, 0:LP].rearrange("p (t q) -> p t q", t=T3)).then_inc(turned_copied, 1)

        eng.wait_ge(k.h_done, 8 * (pos + 1))
        k.ln_copy(eng, pos, 0, 0, 8 * pos)
        with eng.Fori(0, B // 2) as i:
            for half in range(2):
                batch(i * 2 + half, half)

    def dve(eng):
        def batch(b, half):
            eng.wait_ge(projected, 2 * b + 2)
            eng.wait_ge(vproj, b)
            eng.tensor_copy(kT[:, P:], ps[:, 1, 0:LP]).then_inc(copied, 1)
            k.ln_stats(eng, pos, b + 1, 1 - half)
            eng.wait_ge(scored, b + 1)
            eng.tensor_reduce(mx, ps[:, 3:6, 0:2 * P], AX_X, ALU.max).then_inc(maxed, 1)
            eng.wait_ge(maxed, 2 * b + 1)
            eng.wait_ge(exped, 3 * b)
            eng.tensor_scalar(bias, mx, -scale, None, ALU.mult).then_inc(maxed, 1)
            eng.wait_ge(vproj, b + 1)
            eng.wait_ge(mixed, b)
            eng.tensor_copy(vo, ps[:, 2, 0:LP].rearrange("p (t d) -> p t d", t=T3)).then_inc(vcopied, 1)
            k.ln_apply(eng, pos, b + 1, 1 - half)
            eng.wait_ge(exped, 3 * b + 3)
            eng.reciprocal(inv, sums).then_inc(inverted, 1)
            eng.wait_ge(turned, 2 * b + 1)
            eng.tensor_copy(pT[:, 0:2, :], ps[:, 0, 0:2 * P].rearrange("p (t q) -> p t q", t=2)).then_inc(turned_copied, 1)
            eng.wait_ge(mixed, b + 1)
            eng.wait_ge(biased, b + 2)
            eng.wait_ge(inverted, b + 1)
            for t in range(T3):
                r = ROWS[t]
                m = eng.scalar_tensor_tensor(k.tile(b, t, r), ps[0:r, 6, t * D:(t + 1) * D].unsqueeze(1), inv[0:r, t:t + 1],
                                             hb[0:r, half, t:t + 1, :], ALU.mult, ALU.add)
            m.then_inc(k.h_done, 1)

        eng.wait_ge(k.h_done, 8 * (pos + 1))
        k.ln_stats(eng, pos, 0, 0)
        k.ln_apply(eng, pos, 0, 0)
        eng.memset(kT[:, 0:P], 0.0).then_inc(set_up, 1)
        with eng.Fori(0, B // 2) as i:
            for half in range(2):
                batch(i * 2 + half, half)

    def pool(eng):
        eng.wait_ge(k.h_done, 8 * (pos + 1))
        k.ln_power(eng, pos, 0, 0)
        eng.tensor_copy(ident, k.ident[:]).then_inc(set_up, 1)
        eng.memset(mask, 0.0).then_inc(biased, 1)
        eng.wait_ge(biased, 1)
        eng.affine_select(out=mask, in_=mask, compare_op=ALU.is_ge, fill=-1e30, base=0,
                          pattern=[[-1, P]], channel_multiplier=1).then_inc(set_up, 1)
        k.weights_ready(eng, key)
        with eng.Fori(0, B // 2) as i:
            for half in range(2):
                b = i * 2 + half
                eng.wait_ge(k.h_done, i * 2 + 8 * (pos + 1))
                for t in range(T3):
                    m = eng.tensor_tensor(hb[:, half, t:t + 1, :], k.tile(b, t), out_b.unsqueeze(1), ALU.add)
                m.then_inc(biased, 1)
                k.ln_power(eng, pos, b + 1, 1 - half)

    return dict(pe=pe, act=act, dve=dve, pool=pool)


def crossed_attention(k, pos, layer):
    ps, key = k.ps, "l2a"
    H, HD, HV = 8, 16, 32
    w = k.weight(key, key + "_w", [P, 4 * P + H * HD])
    ones = k.weight(key, key + "_ones", [P, 1])
    q, kT = k.carve([P, 2, 2, LP], anew=True), k.carve([P, 2, H, LP])
    v = k.carve([P, 2, T3, H, HV])
    nmax = k.carve([P, 2, T3, P])
    qm = k.carve([P, 2, LP])
    probs = k.carve([P, 3, 2, LP])
    oT = k.carve([P, 2, LP])
    inv, o = k.carve([P, T3, H]), k.carve([P, T3, HD, H])
    s = lambda name: k.phase_sem(f"{key}_{name}")
    set_up, projected, copied, v_copied = s("set_up"), s("projected"), s("qk_copied"), s("v_copied")
    scored, maxed, turned, augmented = s("scores"), s("max"), s("max_turned"), s("q_with_max")
    shifted, exped, mixed, scaled = s("shifted_scores"), s("exp"), s("mixed"), s("scaled")
    gathered, out_turned = s("outputs_copied"), s("outputs_turned")
    ITEMS = 2 * T3 * 2

    def item(n):
        return n // 6, n // 2 % 3, (n % 2 * 2, n % 2 * 2 + 1)

    def pe(eng):
        def project(i, half):
            u = 2 * i + half
            eng.wait_ge(k.ln_xT, u + 9 * pos + 1)
            for j in range(4):
                if half == 0:
                    eng.wait_ge(exped, 2 * ITEMS * i)
                else:
                    eng.wait_ge(copied, 8 * i + j + 1)
                eng.matmul(ps[:, j, 0:LP], w[:, j * P:(j + 1) * P], k.xT[:, half, :], start=True, stop=True).then_inc(projected, 1)
            eng.wait_ge(v_copied, u)
            eng.wait_ge(k.h_done, 2 * i + 8 * (pos + 1))
            for t in range(T3):
                m = eng.matmul(ps[:, 4, t * H * HD:(t + 1) * H * HD], k.xT[:, half, t * P:(t + 1) * P], w[:, 4 * P:],
                               start=True, stop=True)
            m.then_inc(projected, 1)

        def attend(i, half):
            u = 2 * i + half
            eng.wait_ge(copied, 8 * i + 8)
            for n in range(ITEMS):
                g, t, heads = item(n)
                if n < 2:
                    eng.wait_ge(exped, ITEMS * u)
                else:
                    eng.wait_ge(maxed, ITEMS * u + n - 1)
                for j in heads:
                    m = eng.matmul(ps[:, j, 0:L], q[:, half, g, t * P:(t + 1) * P],
                                   kT[:, 1 - half, 4 * g + j, 0:L], start=True, stop=True)
                    if half == 0 and n == 0 and j == 0:
                        m.then_inc(k.xT_used, 2)
                m.then_inc(scored, 1)
            eng.wait_ge(v_copied, 2 * i + 2)
            eng.wait_ge(k.h_done, u + 8 * (pos + 1))
            for g in range(2):
                eng.wait_ge(maxed, ITEMS * u + 6 * g + 6)
                for t in range(T3):
                    m = eng.transpose(ps[:, 4 + g, t * P:(t + 1) * P], nmax[:, g, t, :], k.ident[:])
                m.then_inc(turned, 1)
            eng.wait_ge(maxed, ITEMS * u + ITEMS)
            for n in range(ITEMS + 1):
                if n < ITEMS:
                    g, t, heads = item(n)
                    eng.wait_ge(augmented, 2 * u + g + 1)
                    if n >= 2:
                        eng.wait_ge(exped, ITEMS * u + n - 1)
                    for j in heads:
                        m = eng.matmul(ps[0:ROWS[t], j, 0:L], kT[:, 1 - half, 4 * g + j, t * P:t * P + ROWS[t]],
                                       qm[:, g, 0:L], start=True, stop=True)
                    m.then_inc(shifted, 1)
                if n >= 1:
                    g, t, heads = item(n - 1)
                    eng.wait_ge(exped, ITEMS * u + n)
                    if n == 7:
                        eng.wait_ge(augmented, 2 * u + 2)
                    for j in heads:
                        m = eng.matmul(ps[32 * j:32 * j + 32, 6 - g, 0:L], v[0:ROWS[t], 1 - half, t, 4 * g + j, :],
                                       probs[0:ROWS[t], (n - 1) % 3, j % 2, 0:L], start=(t == 0), stop=(t == T3 - 1))
                    m.then_inc(mixed, 1)
            for g in range(2):
                eng.wait_ge(gathered, 2 * u + g + 1)
                for t in range(T3):
                    m = eng.transpose(ps[0:ROWS[t], 4 + g, t * P:(t + 1) * P], oT[:, g, t * P:t * P + ROWS[t]], k.ident[:])
                m.then_inc(out_turned, 1)

        k.weights_ready(eng, key)
        eng.wait_ge(k.h_done, 8 * (pos + 1))
        k.ln_transpose(eng, pos, 0, 0)
        eng.wait_ge(set_up, 3)
        with eng.Fori(0, B // 2) as i:
            project(i, 0)
            k.ln_transpose(eng, pos, 2 * i + 1, 1)
            project(i, 1)
            attend(i, 0)
            k.ln_transpose(eng, pos, 2 * i + 2, 0)
            attend(i, 1)

    def act(eng):
        def copies(i, half):
            eng.wait_ge(mixed, 2 * ITEMS * i)
            for j in range(4):
                eng.wait_ge(projected, (2 * i + half) * 5 + j + 1)
                if j < 2:
                    m = eng.copy(q[:, half, j, :], ps[:, j, 0:LP])
                else:
                    for n in range(4):
                        rows = slice(32 * n, 32 * n + 32)
                        m = eng.activation(kT[rows, half, 4 * (j - 2) + n, :], ps[rows, j, 0:LP], ACT.Identity, bias=ones[rows, 0:1])
                m.then_inc(copied, 1)

        def exps(i, half):
            u = 2 * i + half
            for n in range(ITEMS):
                g, t, heads = item(n)
                eng.wait_ge(shifted, ITEMS * u + n + 1)
                if n >= 3:
                    eng.wait_ge(mixed, ITEMS * u + n - 2)
                else:
                    eng.wait_ge(mixed, ITEMS * u)
                r = ROWS[t]
                eng.activation(probs[0:r, n % 3, :, 0:L], ps[0:r, heads[0]:heads[0] + 2, 0:L], ACT.Exp,
                               scale=float(D) ** -0.5).then_inc(exped, 1)

        eng.wait_ge(k.h_done, 8 * (pos + 1))
        k.ln_copy(eng, pos, 0, 0, 8 * pos)
        k.weights_ready(eng, key)
        eng.wait_ge(set_up, 3)
        with eng.Fori(0, B // 2) as i:
            copies(i, 0)
            k.ln_copy(eng, pos, 2 * i + 1, 1, 2 * i + 8 * pos)
            copies(i, 1)
            exps(i, 0)
            k.ln_copy(eng, pos, 2 * i + 2, 0, 2 * i + 2 + 8 * pos)
            exps(i, 1)

    def dve(eng):
        def copy_v(i, half):
            eng.wait_ge(projected, (2 * i + half) * 5 + 5)
            eng.wait_ge(mixed, 2 * ITEMS * i)
            for t in range(T3):
                m = eng.tensor_copy(v[:, half, t, :, 0:HD], ps[:, 4, t * H * HD:(t + 1) * H * HD].rearrange("p (h d) -> p h d", h=H))
            m.then_inc(v_copied, 1)

        def gather(i, half, g):
            u = 2 * i + half
            eng.wait_ge(mixed, ITEMS * u + 6 * g + 6)
            eng.wait_ge(out_turned, 2 * u)
            eng.tensor_copy(oT[:, g, 0:L], ps[:, 6 - g, 0:L]).then_inc(gathered, 1)

        def maxima(i, half):
            u = 2 * i + half
            eng.wait_ge(turned, 2 * u)
            for n in range(ITEMS):
                g, t, heads = item(n)
                eng.wait_ge(scored, ITEMS * u + n + 1)
                eng.tensor_reduce(nmax[:, g, t, 32 * heads[0] + HD:32 * heads[1] + HD + 1:32], ps[:, heads[0]:heads[0] + 2, 0:L],
                                  AX_X, ALU.max, negate=True).then_inc(maxed, 1)
            eng.wait_ge(shifted, ITEMS * u)
            for g in range(2):
                eng.wait_ge(turned, 2 * u + g + 1)
                eng.tensor_tensor(qm[:, g, :], q[:, half, g, :], ps[:, 4 + g, 0:LP], ALU.add).then_inc(augmented, 1)

        def finish(i, half):
            u = 2 * i + half
            for g in range(2):
                gather(i, half, g)

            def outputs(t, g):
                return ps[0:ROWS[t], 4 + g, t * P:(t + 1) * P].rearrange("p (h d) -> p d h", h=4)

            for g in range(2):
                eng.wait_ge(out_turned, 2 * u + g + 1)
                for t in range(T3):
                    m = eng.reciprocal(inv[0:ROWS[t], t, 4 * g:4 * g + 4].unsqueeze(1), outputs(t, g)[:, HD:HD + 1, :])
                m.then_inc(scaled, 1)
            eng.wait_ge(scaled, 4 * u + 2)
            for g in range(2):
                for t in range(T3):
                    r = ROWS[t]
                    m = eng.tensor_tensor(o[0:r, t, :, 4 * g:4 * g + 4], outputs(t, g)[:, 0:HD, :],
                                          inv[0:r, t, 4 * g:4 * g + 4].unsqueeze(1).to_broadcast([r, HD, 4]), ALU.mult)
                m.then_inc(scaled, 1)
            eng.wait_ge(scaled, 4 * u + 4)
            for t in range(T3):
                r = ROWS[t]
                at = k.tile(i + (B // 2) * half, t, r)
                m = eng.tensor_tensor(at, at, o[0:r, t].rearrange("p d h -> p (d h)").unsqueeze(1), ALU.add)
            m.then_inc(k.h_done, 1)

        eng.wait_ge(k.h_done, 8 * (pos + 1))
        k.ln_stats(eng, pos, 0, 0)
        k.ln_apply(eng, pos, 0, 0)
        eng.memset(v, 0.0).then_inc(set_up, 1)
        eng.wait_ge(set_up, 1)
        for half in range(2):
            m = eng.memset(v[:, half, :, :, HD:HD + 1], 1.0)
        m.then_inc(set_up, 1)
        eng.memset(nmax, 0.0)
        eng.memset(kT, 0.0).then_inc(set_up, 1)
        eng.wait_ge(set_up, 3)
        with eng.Fori(0, B // 2) as i:
            k.ln_stats(eng, pos, 2 * i + 1, 1, i + B // 2)
            copy_v(i, 0)
            k.ln_apply(eng, pos, 2 * i + 1, 1, i + B // 2)
            copy_v(i, 1)
            maxima(i, 0)
            k.ln_stats(eng, pos, 2 * i + 2, 0, i + 1)
            k.ln_apply(eng, pos, 2 * i + 2, 0, i + 1)
            finish(i, 0)
            maxima(i, 1)
            finish(i, 1)

    def pool(eng):
        eng.wait_ge(k.h_done, 8 * (pos + 1))
        k.ln_power(eng, pos, 0, 0)
        with eng.Fori(0, B // 2) as i:
            k.ln_power(eng, pos, 2 * i + 1, 1)
            k.ln_power(eng, pos, 2 * i + 2, 0)

    return dict(pe=pe, act=act, dve=dve, pool=pool)


def delta_attention(k, pos, layer):
    ps, key = k.ps, "l0a"
    C, NC, NP = 64, LP // 64, 4
    DH = 64
    room = Room(k.w_l1)
    w_hid = k.weight(key, key + "_hid", [P, 2 * P], room=room)
    w_k = k.weight(key, key + "_wk", [DH, 2 * 256], room=room)
    w_q = k.weight(key, key + "_wq", [P, 2 * 256], room=room)
    w_v = k.weight(key, key + "_wv", [P, 2 * 256], room=room)
    w_gates = k.weight(key, key + "_gates", [P, 2 * 8], room=room)
    w_out = k.weight(key, key + "_out", [P, NP * D], room=room)
    out_b = k.weight(key, key + "_out_b", [P, D], broadcast=True, room=room)
    w_vv = k.weight(key, key + "_vv", [P, 4 * (P + DH)], room=room)
    conv = k.weight(key, key + "_conv", [P, 5], room=room)
    consts = k.weight(key, key + "_consts", [P, 3 * C + 4 * P], room=room)
    norms = room.lay([P, 4, 256])
    for par in range(2):
        k.load(key, norms[64 * par:64 * par + 64].rearrange("p a b -> p (a b)"), k.W[key + "_norms"][par].partition_broadcast(64))
    eye, before, future = (consts[:, j * C:(j + 1) * C] for j in range(3))
    c_before, c_behind, c_head, c_token = (consts[:, 3 * C + j * P:3 * C + (j + 1) * P] for j in range(4))
    V, lat, Kdec = (k.carve([P, NC, NP, C], anew=j == 0) for j in range(3))
    K, Q = k.carve([P, 2, NP, C]), k.carve([P, 2, NP, C])
    KB, QB = k.carve([P, 2, NP, P]), k.carve([P, 2, NP, P])
    eK, eQ = k.carve([P, 2, NP, P]), k.carve([P, 2, NP, P])
    xc, sK, sV, sB = (k.carve([P, LP]) for _ in range(4))
    hb = k.carve([P, T3, D])
    ssq, ve, rs = k.carve([P, 2, NC]), k.carve([P, 3, 4]), k.carve([P, 3, 4])
    z = k.carve([P, 3, NC, 8])
    zc = k.carve([P, NC, 8])
    e, m2e, la, coef, n2, rn = (k.carve([P, NC, NP]) for _ in range(6))
    cum = k.carve([P, 3, NC, NP])
    sums, wvv = k.carve([P, 2]), k.carve([P, C])
    tap = k.carve([P, 1])
    room2 = Room(k.w_l2)

    def lay(*shape):
        return room2.lay([P] + list(shape))

    KQ, Rt, PT = lay(3, 2, NP, 2 * C), lay(3, 2, NP, C), lay(3, 2, NP, C)
    BQ, DT = lay(2, NP, 2 * C), lay(2, NP, C)
    XX = lay(2, 2, NP, P)
    rr, tmp, U = lay(NP, C), lay(NP, C), lay(NP, C)
    S, yT = room.lay([P, NP, C]), room.lay([P, NP, LP])
    sq = room.lay([P, 2, NP, C])
    mask, ident = lay(NP * C // 2).bitcast(BF16), lay(P // 2).bitcast(BF16)
    s = lambda name: k.phase_sem(f"{key}_{name}")
    set_up, conved, hid, act_hid, vproj = s("set_up"), s("conv"), s("hid"), s("hid_silu"), s("vh_hid")
    gates, projected, kq_copied, v_copied = s("gates"), s("kqv"), s("kq_copied"), s("v_copied")
    sumsq, varred, rstd, normed = s("sumsq"), s("variance"), s("rstd"), s("k_steps")
    softened, clipped, logged, cumul, cumexp = s("softplus"), s("gate_steps"), s("log_decay"), s("cumulated"), s("cum_exp")
    norm_in, norm_out, pooled = s("k_norm_in"), s("k_norm"), s("pool_steps")
    turned, copied_a, copied_d = s("turned"), s("turned_act"), s("turned_dve")
    zsum, decays, raw, scaled, n_turned, x_ready = s("decay_sums"), s("decays"), s("raw_NP"), s("scaled_NP"), s("N_turned"), s("N_ready")
    squared, applied, xt_copied, level = s("squared"), s("R_product"), s("X_copied"), s("R_added")
    ks, rr_done, us, u_copied, new, y_copied, s_done = s("KS"), s("rhs_steps"), s("U"), s("U_copied"), s("new_state"), s("y_copied"), s("S_steps")
    out_done, biased = s("out"), s("h_biased")
    SU = 1 + 2 * NC

    def quads(eng, out, lhsT, rhs, start=True, stop=True):
        for p in range(NP):
            for h in (slice(0, 64), slice(64, 128)):
                m = eng.matmul(out(p)[h], lhsT(p)[h], rhs(p)[h], start=start, stop=stop)
        return m

    def wide(bank, n=2 * C):
        return ps[:, bank, 0:NP * n].rearrange("p (a b) -> p a b", a=NP)

    def until(eng, sem, value):
        if not isinstance(value, int) or value > 0:
            eng.wait_ge(sem, value)

    AHEAD = {(0, 0): "hidden", (0, 1): "gates", (1, 0): "chunk0", (1, 1): "chunk1", (2, 0): "sums",
             (2, 1): "variance", (3, 0): "norm", (3, 1): "shift", (4, 0): "length", (4, 1): "scale"}
    STEPS = list(AHEAD.values())

    def following(b, m):
        return (b, m + 1) if m < 2 else (b + 1, 0)

    def previous(b, m):
        return (b, m - 1) if m > 0 else (b - 1, 2)

    def pe(eng):
        def wait(sem, value):
            if not isinstance(value, int):
                k.wait_apart(eng, sem, value)
            elif value > 0:
                eng.wait_ge(sem, value)

        def ahead(bt, mt, step):
            t = 3 * bt + mt
            if step == "hidden" and mt == 0:
                until(eng, conved, 4 * bt + 4)
                until(eng, decays, 2 * t)
                until(eng, varred, t)
                eng.matmul(ps[:, 4, 0:LP], w_hid[:, 0:P], xc, start=True, stop=True)
                eng.matmul(ps[:, 7, 0:LP], w_hid[:, P:], xc, start=True, stop=True).then_inc(hid, 1)
            if step == "gates":
                if mt == 0:
                    wait(act_hid, 2 * bt + 1)
                    eng.matmul(ps[0:64, 4, 0:LP], wvv[64:128], sV[64:128], start=True, stop=True).then_inc(vproj, 1)
                elif mt == 2:
                    wait(k.ln_xT, 9 * pos + bt + 2)
                    wait(varred, t)
                else:
                    wait(varred, t)
                for c in range(2 * mt, 2 * mt + 2):
                    for par in range(2):
                        i = eng.matmul(ps[64 * par:64 * par + 64, 7, c % 2 * 8:c % 2 * 8 + 8], sB[:, c * C:(c + 1) * C],
                                       w_gates[:, par * 8:par * 8 + 8], start=True, stop=True)
                i.then_inc(gates, 1)
            if step in ("chunk0", "chunk1"):
                c = 2 * mt + int(step[-1])
                if step == "chunk0":
                    wait(act_hid, 2 * bt + 2)
                    wait(decays, 2 * t)
                    wait(clipped, 5 * t + 2)
                else:
                    wait(kq_copied, bt * NC + c)
                    wait(v_copied, bt * NC + c)
                for at, x_, w_ in ((ps[:, 4, 0:256], sK[0:64], w_k), (ps[:, 4, 256:512], xc, w_q), (ps[:, 7, 0:256], sV, w_v)):
                    for par in range(2):
                        i = eng.matmul(at[64 * par:64 * par + 64], x_[:, c * C:(c + 1) * C], w_[:, 256 * par:256 * par + 256],
                                       start=True, stop=True)
                i.then_inc(projected, 1)
            if step == "sums":
                c = 2 * mt
                until(eng, kq_copied, 2 * t + 2)
                until(eng, v_copied, 2 * t + 2)
                for j in range(2):
                    i = eng.matmul(ps[:, 7, 2 * j:2 * j + 2], c_token, ssq[:, j, c:c + 2], start=True, stop=True)
                i.then_inc(sumsq, 1)
                until(eng, logged, t + 1)
                for j, m_ in enumerate((c_before, c_behind, c_head)):
                    i = eng.matmul(ps[:, 4, 8 * j:8 * j + 8], m_, la[:, c:c + 2].rearrange("p a b -> p (a b)"), start=True, stop=True)
                i.then_inc(cumul, 1)

        def prepare(b, m):
            t = 3 * b + m
            for x in range(2):
                n = b * NC + 2 * m + x
                if x == 0:
                    until(eng, pooled, 4 * t + 4)
                    until(eng, normed, 10 * t + 10)
                    wait(level, 10 * t)
                    wait(xt_copied, 10 * t)
                for bank, both, diagonals in ((x, KB, eK), (2 + x, QB, eQ)):
                    for p in range(NP):
                        i = eng.matmul(wide(bank)[:, p, :], both[:, x, p, :], diagonals[:, x, p, :], start=True, stop=True)
                i.then_inc(turned, 1)
            until(eng, cumexp, t + 1)
            if m == 1:
                until(eng, k.h_done, b + 8 * (pos + 1))
            for x in range(2):
                z_at = ps[:, 4, x * 256:x * 256 + 256]
                eng.matmul(z_at, c_behind, lat[:, 2 * m + x].rearrange("p a b -> p (a b)"), start=True, stop=False)
                eng.matmul(z_at, ident, mask, start=False, stop=True).then_inc(zsum, 1)
            for x in range(2):
                n = b * NC + 2 * m + x
                wait(copied_a, n + 1)
                wait(copied_d, n + 1)
                quads(eng, lambda p: wide(x)[:, p, :], lambda p: KQ[:, m, x, p, 0:C], lambda p: BQ[:, x, p, :]).then_inc(raw, 1)
            for x in range(2):
                wait(scaled, 3 * (b * NC + 2 * m + x) + 3)
                for p in range(NP):
                    i = eng.matmul(wide(2 + x)[:, p, :], XX[:, x, 0, p, :], k.ident[:], start=True, stop=True)
                i.then_inc(n_turned, 1)

        def square(b, m, lv, x):
            n, t = b * NC + 2 * m + x, 3 * b + m
            if lv == 0:
                wait(x_ready, n + 1)
            else:
                wait(xt_copied, 10 * t + 2 * (lv - 1) + x + 1)
                until(eng, level, 10 * t + 2 * (lv - 1) + x)
                for p in range(NP):
                    i = eng.matmul(ps[:, 6, x * 256 + p * C:x * 256 + (p + 1) * C], XX[:, x, 1, p, :], Rt[:, m, x, p, :],
                                   start=True, stop=True)
                i.then_inc(applied, 1)
            if lv < 5:
                for j in range(2) if lv < 4 else (1,):
                    for p in range(NP):
                        i = eng.matmul(wide(2 * x + j)[:, p, :], XX[:, x, 1 - j, p, :], XX[:, x, j, p, :], start=True, stop=True)
                i.then_inc(squared, 1)

        def state(b, m, j):
            x = j // 3
            n = b * NC + 2 * m + x
            kq, xr = lambda lo: lambda p: KQ[:, m, x, p, lo:lo + C], lambda p: Rt[:, m, x, p, :]
            if j % 3 == 0:
                wait(s_done, SU * b + 1 + 2 * (2 * m + x))
                quads(eng, lambda p: wide(5, C)[:, p, :], kq(0), lambda p: S[:, p, :]).then_inc(ks, 1)
            elif j % 3 == 1:
                wait(rr_done, 2 * n + 2)
                quads(eng, lambda p: wide(5, C)[:, p, :], xr, lambda p: rr[:, p, :]).then_inc(us, 1)
            else:
                wait(u_copied, n + 1)
                wait(y_copied, n)
                for p in range(NP):
                    for h in (slice(0, 64), slice(64, 128)):
                        at = ps[h, 5, 256 + p * C:256 + (p + 1) * C]
                        eng.matmul(at, S[h, p, :], KQ[h, m, x, p, C:], start=True, stop=False)
                        eng.matmul(at, U[h, p, :], PT[h, m, x, p, :], start=False, stop=True)
                quads(eng, lambda p: wide(5, C)[:, p, :], lambda p: Kdec[:, 2 * m + x, p, :], lambda p: U[:, p, :]).then_inc(new, 1)

        k.weights_ready(eng, key)
        eng.wait_ge(k.h_done, 8 * (pos + 1))
        for j in range(4):
            at = j * (P + DH)
            m = eng.matmul(ps[:, 6, 0:DH], w_vv[:, at:at + P], w_vv[:, at + P:at + P + DH], start=(j == 0), stop=(j == 3))
        m.then_inc(set_up, 1)
        k.ln_transpose(eng, pos, 0, 0)
        eng.wait_ge(set_up, 10)
        def output(b):
            eng.wait_ge(y_copied, b * NC + NC)
            for t in range(T3):
                for p in range(NP):
                    i = eng.matmul(ps[:, 4, t * D:(t + 1) * D], yT[:, p, t * P:(t + 1) * P], w_out[:, p * D:(p + 1) * D],
                                   start=(p == 0), stop=(p == NP - 1))
            i.then_inc(out_done, 1)

        def batch(b, first=False):
            for m in range(3):
                prepare(b, m)
                for lv in range(6):
                    for x in range(2):
                        square(b, m, lv, x)
                        if (lv, x) in AHEAD:
                            ahead(*following(b, m), AHEAD[lv, x])
                    if not (first and m == 0):
                        state(*previous(b, m), lv)
                if m == 0 and not first:
                    output(b - 1)
                if m == 0:
                    until(eng, varred, 3 * b + 2)
                    k.ln_transpose(eng, pos, b + 1, 0)

        for step in STEPS:
            ahead(0, 0, step)
        batch(0, first=True)
        with eng.Fori(1, B) as b:
            batch(b)
        for j in range(6):
            state(B - 1, 2, j)
        eng.wait_ge(cumexp, 3 * B + 1)
        output(B - 1)

    def act(eng):
        def ahead(bt, mt, step):
            t = 3 * bt + mt
            if step == "hidden" and mt == 0:
                until(eng, hid, bt + 1)
                eng.activation(sK[0:64], ps[0:64, 4, 0:LP], ACT.Silu)
                eng.activation(sV[64:128], ps[64:128, 4, 0:LP], ACT.Silu)
                eng.activation(sB, ps[:, 7, 0:LP], ACT.Silu).then_inc(act_hid, 1)
            if step == "gates":
                if mt == 0:
                    until(eng, vproj, bt + 1)
                    eng.activation(sV[0:64], ps[0:64, 4, 0:LP], ACT.Silu).then_inc(act_hid, 1)
                cs = slice(2 * mt, 2 * mt + 2)
                until(eng, gates, t + 1)
                until(eng, clipped, 5 * t)
                eng.activation(z[:, 0, cs], ps[:, 7, 0:16].rearrange("p (a b) -> p a b", a=2), ACT.Abs).then_inc(softened, 1)
                until(eng, softened, 3 * t + 1)
                eng.activation(z[:, 1, cs], z[:, 0, cs], ACT.Exp, scale=-1.0).then_inc(softened, 1)
                until(eng, softened, 3 * t + 2)
                eng.activation(z[:, 2, cs], z[:, 1, cs], ACT.Ln, bias=1.0).then_inc(softened, 1)
            if step in ("chunk0", "chunk1"):
                c = 2 * mt + int(step[-1])
                until(eng, projected, bt * NC + c + 1)
                until(eng, new, 2 * t - 4)
                until(eng, normed, 10 * t)
                for j, dst in enumerate((K, Q)):
                    at = ps[:, 4, j * 256:(j + 1) * 256]
                    junk = (sq[:, c % 2], Kdec[:, c])[j]
                    eng.activation(junk.rearrange("p a b -> p (a b)"), at, ACT.Square, accum_out=ssq[:, j, c:c + 1])
                    i = eng.copy(dst[:, c % 2].rearrange("p a b -> p (a b)"), at)
                i.then_inc(kq_copied, 1)
            if step == "sums":
                until(eng, cumul, t + 1)
                until(eng, s_done, SU * bt + 4 * mt - 12 if mt else 0)
                eng.activation(cum[:, :, 2 * mt:2 * mt + 2], ps[:, 4, 0:24].rearrange("p (a b c) -> p a b c", a=3, b=2), ACT.Exp).then_inc(cumexp, 1)

        def prepare(b, m):
            for x in range(2):
                n = b * NC + 2 * m + x
                eng.wait_ge(turned, n + 1)
                eng.copy(KQ[:, m, x, :, 0:C], wide(x)[:, :, 0:C])
                eng.copy(BQ[:, x, :, 0:C], wide(x)[:, :, C:]).then_inc(copied_a, 1)
            for x in range(2):
                eng.wait_ge(zsum, b * NC + 2 * m + 2)
                eng.activation(DT[:, x], wide_z(x), ACT.Exp).then_inc(decays, 1)
            for x in range(2):
                eng.wait_ge(n_turned, b * NC + 2 * m + x + 1)
                eng.copy(XX[:, x, 1], wide(2 + x)).then_inc(x_ready, 1)

        def wide_z(x):
            return ps[:, 4, x * 256:x * 256 + 256].rearrange("p (a b) -> p a b", a=NP)

        def state(b, m, j):
            x = j // 3
            n = b * NC + 2 * m + x
            if j % 3 == 1:
                eng.wait_ge(us, n + 1)
                eng.copy(U, wide(5, C)).then_inc(u_copied, 1)

        eng.wait_ge(k.h_done, 8 * (pos + 1))
        k.ln_copy(eng, pos, 0, 0, 8 * pos)
        eng.wait_ge(set_up, 1)
        eng.copy(wvv[64:128], ps[64:128, 6, 0:DH]).then_inc(set_up, 1)
        def batch(b, first=False):
            for m in range(3):
                prepare(b, m)
                for lv in range(6):
                    for x in range(2):
                        if lv < 5:
                            eng.wait_ge(squared, b * 30 + m * 10 + lv * 2 + x + 1)
                            j = 0 if lv < 4 else 1
                            eng.copy(XX[:, x, j:], ps[:, 2 * x + j:2 * x + 2, :].rearrange("p j (a b) -> p j a b", a=NP)).then_inc(xt_copied, 1)
                        if (lv, x) in AHEAD:
                            ahead(*following(b, m), AHEAD[lv, x])
                    if not (first and m == 0):
                        state(*previous(b, m), lv)
                if m == 0:
                    k.ln_copy(eng, pos, b + 1, 0, b + 1 + 8 * pos)

        for step in STEPS:
            ahead(0, 0, step)
        batch(0, first=True)
        with eng.Fori(1, B) as b:
            batch(b)
        for j in range(6):
            state(B - 1, 2, j)

    def dve(eng):
        def per_token(arr):
            return arr.unsqueeze(3).to_broadcast([P, 2, NP, C])

        def convolve(b):
            until(eng, k.ln_xT, b + 9 * pos + 1)
            until(eng, projected, b * NC)
            x_ = k.xT[:, 0, :]
            eng.tensor_scalar(xc, x_, tap[:, 0:1], conv[:, 4:5], ALU.mult, ALU.add).then_inc(conved, 1)
            for j in range(1, 4):
                until(eng, conved, 4 * b + j)
                eng.scalar_tensor_tensor(xc[:, j:], x_[:, 0:LP - j], conv[:, 3 - j:4 - j], xc[:, j:], ALU.mult, ALU.add).then_inc(conved, 1)
            until(eng, conved, 4 * b + 4)
            eng.sem_inc(k.xT_used, 1)

        def ahead(bt, mt, step):
            t = 3 * bt + mt
            cs = slice(2 * mt, 2 * mt + 2)
            if step in ("chunk0", "chunk1"):
                c = 2 * mt + int(step[-1])
                if step == "chunk0":
                    at = ps[:, 7, 0:16].rearrange("p (a b) -> p a b", a=2)
                    until(eng, softened, 3 * t + 1)
                    eng.tensor_scalar(zc[:, cs, 0:4], at[:, :, 0:4], 0.0, None, ALU.max).then_inc(clipped, 1)
                    eng.tensor_scalar(zc[:, cs, 4:8], at[:, :, 4:8], 0.0, None, ALU.min).then_inc(clipped, 1)
                    until(eng, softened, 3 * t + 3)
                    until(eng, clipped, 5 * t + 2)
                    until(eng, cumul, t)
                    eng.tensor_tensor(la[:, cs], zc[:, cs, 4:8], z[:, 2, cs, 4:8], ALU.subtract).then_inc(logged, 1)
                    eng.tensor_tensor(e[:, cs], zc[:, cs, 0:4], z[:, 2, cs, 0:4], ALU.add).then_inc(clipped, 1)
                    until(eng, clipped, 5 * t + 3)
                    eng.tensor_scalar(m2e[:, cs], e[:, cs], -0.2, None, ALU.mult).then_inc(clipped, 1)
                    until(eng, clipped, 5 * t + 4)
                    eng.tensor_scalar(e[:, cs], e[:, cs], 0.1, None, ALU.mult).then_inc(clipped, 1)
                until(eng, projected, bt * NC + c + 1)
                eng.tensor_copy(V[:, c].rearrange("p a b -> p (a b)"), ps[:, 7, 0:256]).then_inc(v_copied, 1)
            if step == "sums":
                until(eng, sumsq, t + 1)
                eng.tensor_scalar(ve[:, mt], ps[:, 7, 0:4], 1.0 / 512, EPS, ALU.mult, ALU.add).then_inc(varred, 1)
            if step == "norm":
                until(eng, rstd, t + 1)
                for j, arr in enumerate((K, Q)):
                    for c in range(2 * mt, 2 * mt + 2):
                        at = arr[:, c % 2].rearrange("p a b -> p (a b)")
                        i = eng.scalar_tensor_tensor(at, at, rs[:, mt, 2 * j + c % 2:2 * j + c % 2 + 1], norms[:, 2 * j, :], ALU.mult, ALU.mult)
                    i.then_inc(normed, 1)
            if step == "shift":
                until(eng, normed, 10 * t + 2)
                at = K.rearrange("p c a d -> p c (a d)")
                eng.tensor_tensor(at, at, norms[:, 1, :].unsqueeze(1).to_broadcast([P, 2, 256]), ALU.add).then_inc(normed, 1)
                for h in (slice(0, 64), slice(64, 128)):
                    b_ = norms[h, 3, :].rearrange("p (a d) -> p a d", a=NP).unsqueeze(1).to_broadcast([64, 2, NP, C])
                    i = eng.tensor_tensor(QB[h, :, :, h], Q[h], b_, ALU.add)
                i.then_inc(normed, 1)
            if step == "length":
                until(eng, normed, 10 * t + 4)
                eng.tensor_tensor(sq, K, K, ALU.mult).then_inc(normed, 1)
                until(eng, normed, 10 * t + 5)
                eng.tensor_reduce(n2[:, cs], sq, AX_X, ALU.add).then_inc(normed, 1)
                until(eng, normed, 10 * t + 6)
                eng.tensor_scalar(n2[:, cs], n2[:, cs], 1e-24, None, ALU.max).then_inc(norm_in, 1)
            if step == "scale":
                until(eng, norm_out, t + 1)
                eng.tensor_tensor(K, K, per_token(rn[:, cs]), ALU.mult).then_inc(normed, 1)
                until(eng, cumexp, t + 1)
                eng.tensor_tensor(coef[:, cs], m2e[:, cs], cum[:, 0, cs], ALU.mult).then_inc(normed, 1)
                until(eng, normed, 10 * t + 8)
                eng.tensor_tensor(Kdec[:, cs], K, per_token(cum[:, 1, cs]), ALU.mult).then_inc(normed, 1)
                for h in (slice(0, 64), slice(64, 128)):
                    i = eng.tensor_copy(KB[h, :, :, h], K[h])
                i.then_inc(normed, 1)

        def prepare(b, m):
            for x in range(2):
                n = b * NC + 2 * m + x
                eng.wait_ge(turned, n + 1)
                eng.tensor_copy(BQ[:, x, :, C:], wide(2 + x)[:, :, 0:C])
                eng.tensor_copy(KQ[:, m, x, :, C:], wide(2 + x)[:, :, C:]).then_inc(copied_d, 1)
            for x in range(2):
                n = b * NC + 2 * m + x
                eng.wait_ge(raw, n + 1)
                eng.wait_ge(decays, n + 1)
                eng.wait_ge(applied, b * 30 + m * 10)
                eng.tensor_tensor(Rt[:, m, x], wide(x)[:, :, 0:C], DT[:, x], ALU.mult)
                eng.tensor_tensor(PT[:, m, x], wide(x)[:, :, C:], DT[:, x], ALU.mult).then_inc(scaled, 1)
                eng.wait_ge(scaled, 3 * n + 1)
                for h in range(2):
                    at = slice(C * h, C * h + C)
                    i = eng.tensor_copy(XX[at, x, 0, :, at], Rt[at, m, x])
                i.then_inc(scaled, 1)
                eng.wait_ge(scaled, 3 * n + 2)
                eng.tensor_tensor(Rt[:, m, x], Rt[:, m, x], eye.unsqueeze(1).to_broadcast([P, NP, C]), ALU.add).then_inc(scaled, 1)

        def state(b, m, j):
            x = j // 3
            c = 2 * m + x
            n = b * NC + c
            if c == 0 and j == 0:
                until(eng, new, n)
                until(eng, s_done, SU * b)
                eng.memset(S, 0.0).then_inc(s_done, 1)
            if j % 3 == 0:
                eng.wait_ge(ks, n + 1)
                eng.tensor_tensor(tmp, wide(5, C), coef[:, c].unsqueeze(2).to_broadcast([P, NP, C]), ALU.mult).then_inc(rr_done, 1)
                eng.wait_ge(rr_done, 2 * n + 1)
                eng.wait_ge(us, n)
                eng.tensor_tensor(rr, tmp, V[:, c], ALU.add).then_inc(rr_done, 1)
            elif j % 3 == 2:
                at = SU * b + 1 + 2 * c
                eng.wait_ge(new, n + 1)
                if c == 0:
                    until(eng, out_done, b)
                eng.tensor_copy(yT[:, :, c * C:(c + 1) * C], ps[:, 5, 256:512].rearrange("p (a b) -> p a b", a=NP)).then_inc(y_copied, 1)
                eng.tensor_tensor(S, S, cum[:, 2, c].unsqueeze(2).to_broadcast([P, NP, C]), ALU.mult).then_inc(s_done, 1)
                eng.wait_ge(s_done, at + 1)
                eng.tensor_tensor(S, S, wide(5, C), ALU.add).then_inc(s_done, 1)

        eng.wait_ge(k.h_done, 8 * (pos + 1))
        k.ln_stats(eng, pos, 0, 0)
        k.ln_apply(eng, pos, 0, 0)
        k.weights_ready(eng, key)
        eng.tensor_scalar(tap, conv[:, 3:4], 1.0, None, ALU.add)
        eng.tensor_copy(mask.rearrange("p (a b) -> p a b", a=NP), future.unsqueeze(1).to_broadcast([P, NP, C]))
        eng.tensor_copy(ident, k.ident[:]).then_inc(set_up, 1)
        eng.tensor_reduce(sums[0:DH, 0:1], w_k[:], AX_X, ALU.add).then_inc(set_up, 1)
        eng.tensor_reduce(sums[:, 1:2], w_q[:], AX_X, ALU.add).then_inc(set_up, 1)
        eng.wait_ge(set_up, 5)
        eng.tensor_scalar(sums[0:DH, 0:1], sums[0:DH, 0:1], 1.0 / 512, None, ALU.mult).then_inc(set_up, 1)
        eng.tensor_scalar(sums[:, 1:2], sums[:, 1:2], 1.0 / 512, None, ALU.mult).then_inc(set_up, 1)
        eng.wait_ge(set_up, 7)
        eng.tensor_scalar(w_k[:], w_k[:], sums[0:DH, 0:1], None, ALU.subtract).then_inc(set_up, 1)
        eng.tensor_scalar(w_q[:], w_q[:], sums[:, 1:2], None, ALU.subtract).then_inc(set_up, 1)
        eng.memset(XX, 0.0)
        eng.memset(KB, 0.0)
        eng.memset(QB, 0.0)
        for at in (eK, eQ):
            i = eng.tensor_copy(at[:, :, :, 0:C], eye.unsqueeze(1).unsqueeze(1).to_broadcast([P, 2, NP, C]))
        i.then_inc(set_up, 1)
        eng.wait_ge(set_up, 10)
        def finish(b):
            eng.wait_ge(out_done, b + 1)
            eng.wait_ge(biased, b + 1)
            for t in range(T3):
                r = ROWS[t]
                i = eng.tensor_tensor(k.tile(b, t, r), hb[0:r, t:t + 1, :], ps[0:r, 4, t * D:(t + 1) * D].unsqueeze(1), ALU.add)
            i.then_inc(k.h_done, 1)

        def batch(b, first=False):
            for m in range(3):
                prepare(b, m)
                for lv in range(6):
                    for x in range(2):
                        if lv > 0:
                            eng.wait_ge(applied, b * 30 + m * 10 + (lv - 1) * 2 + x + 1)
                            at = ps[:, 6, x * 256:(x + 1) * 256].rearrange("p (a b) -> p a b", a=NP)
                            eng.tensor_tensor(Rt[:, m, x], Rt[:, m, x], at, ALU.add).then_inc(level, 1)
                        if (lv, x) in AHEAD:
                            ahead(*following(b, m), AHEAD[lv, x])
                    if not (first and m == 0):
                        state(*previous(b, m), lv)
                    if m == 0 and lv == 1:
                        k.ln_stats(eng, pos, b + 1, 0)
                    if m == 0 and lv == 5:
                        k.ln_apply(eng, pos, b + 1, 0)
                if m == 0 and not first:
                    finish(b - 1)
                if m == 1:
                    convolve(b + 1)

        convolve(0)
        for step in STEPS:
            ahead(0, 0, step)
        batch(0, first=True)
        with eng.Fori(1, B) as b:
            batch(b)
        for j in range(6):
            state(B - 1, 2, j)
        finish(B - 1)

    def pool(eng):
        def spread(arr):
            return arr.unsqueeze(3).to_broadcast([P, 2, NP, C])

        def const(arr):
            return arr.unsqueeze(1).unsqueeze(1).to_broadcast([P, 2, NP, C])

        def ahead(bt, mt):
            t = 3 * bt + mt
            cs = slice(2 * mt, 2 * mt + 2)
            until(eng, logged, t + 1)
            until(eng, new, 2 * t - 4)
            eng.tensor_tensor(lat[:, cs], spread(la[:, cs]), const(before), ALU.mult).then_inc(pooled, 1)
            until(eng, varred, t + 1)
            eng.tensor_tensor(rs[:, mt], ve[:, mt], k.neghalf[:, 0:4], ALU.pow).then_inc(rstd, 1)
            until(eng, clipped, 5 * t + 5)
            until(eng, turned, 2 * t)
            eng.tensor_tensor(eK[:, :, :, C:], spread(m2e[:, cs]), const(eye), ALU.mult).then_inc(pooled, 1)
            until(eng, norm_in, t + 1)
            eng.tensor_tensor(rn[:, cs].rearrange("p a b -> p (a b)"), n2[:, cs].rearrange("p a b -> p (a b)"), k.neghalf[:, 0:8],
                              ALU.pow).then_inc(norm_out, 1)
            until(eng, cumexp, t + 1)
            eng.tensor_tensor(eQ[:, :, :, C:], spread(cum[:, 0, cs]), const(eye), ALU.mult).then_inc(pooled, 1)
            until(eng, v_copied, 2 * t + 2)
            eng.tensor_tensor(V[:, cs], V[:, cs], spread(e[:, cs]), ALU.mult).then_inc(pooled, 1)

        def batch(b, first=False):
            ahead(b, 1)
            k.ln_power(eng, pos, b + 1, 0)
            ahead(b, 2)
            until(eng, k.h_done, b + 8 * (pos + 1))
            for t in range(T3):
                i = eng.tensor_tensor(hb[:, t:t + 1, :], k.tile(b, t), out_b.unsqueeze(1), ALU.add)
            i.then_inc(biased, 1)
            ahead(b + 1, 0)

        eng.wait_ge(k.h_done, 8 * (pos + 1))
        k.ln_power(eng, pos, 0, 0)
        k.weights_ready(eng, key)
        ahead(0, 0)
        batch(0)
        with eng.Fori(1, B) as b:
            batch(b)

    return dict(pe=pe, act=act, dve=dve, pool=pool)


def emit(nc, W, out, active):
    with ExitStack() as ctx:
        k = Core(nc, ctx, W, out)
        phases = []
        for pos, layer in enumerate([None] + list(active), -1):
            with ExitStack() as k.phase_sems:
                phases.append(tdnn(k) if layer is None else PHASES[layer](k, pos, layer))
        block = ctx.enter_context(nc.Block())

        @block.sync
        def _(sp):
            for p in phases:
                if "sync" in p:
                    p["sync"](sp)
            for key, dst, src, after in k.loads:
                if after is not None:
                    sp.wait_ge(k.phase_begun, after + 1)
                sp.dma_start(dst, src).then_inc(k.w_sem[key][0], 16)
            with sp.Fori(0, B) as b:
                sp.wait_ge(k.h_done, b + (8 * len(active) + 1))
                sp.dma_start(out[bass.ds(b, 1), 0:2 * P, :].rearrange("a (t p) d -> p (a t) d", p=P),
                             k.h[:, bass.ds(b * T3, 2), :]).then_inc(k.out_written, 16)
                sp.dma_start(out[bass.ds(b, 1), 2 * P:L, :].rearrange("a p d -> p a d"),
                             k.tile(b, 2, ROWS[2])).then_inc(k.out_written, 16)
            sp.wait_ge(k.out_written, 2 * 16 * B)

        @block.tensor
        def _(pe):
            for number, p in enumerate(phases):
                if number > 0:
                    k.next_phase("pe", pe, number - 1)
                p["pe"](pe)

        @block.scalar
        def _(act):
            for number, p in enumerate(phases):
                if number > 0:
                    k.next_phase("act", act, number - 1)
                p["act"](act)

        @block.vector
        def _(dve):
            for number, p in enumerate(phases):
                if number > 0:
                    k.next_phase("dve", dve, number - 1)
                p["dve"](dve)

        @block.gpsimd
        def _(pool):
            pool.memset(k.ident[:], 1.0).then_inc(k.const_ready, 1)
            pool.wait_ge(k.const_ready, 1)
            pool.memset(k.neghalf[:], -0.5)
            pool.affine_select(out=k.ident[:], in_=k.ident[:], compare_op=ALU.is_equal, fill=0.0, base=0,
                               pattern=[[-1, P]], channel_multiplier=1).then_inc(k.const_ready, 1)
            for number, p in enumerate(phases):
                if number > 0:
                    k.next_phase("pool", pool, number - 1)
                p["pool"](pool)


PHASES = {L0A: delta_attention, L1A: window_attention, L2A: crossed_attention, L3A: linear_attention, L0F: experts, L1F: experts, L2F: experts, L3F: experts}


def laid_out_delta(q):
    import numpy as np
    cat = np.concatenate
    heads = lambda w: w.reshape(w.shape[0], 4, 2, 64).transpose(0, 2, 1, 3).reshape(w.shape[0], -1)
    r = {"l0a_hid": cat([q["Mk_W2"].T, q["Mv_W2"].T, q["Meta_W2"].T, q["Malpha_W2"].T], 1),
         "l0a_wk": heads(q["Mk_W1"].T), "l0a_wq": heads(q["Wq"].T),
         "l0a_wv": heads(cat([q["Mvh_W1"].T, q["Mv_W1"].T])),
         "l0a_out": q["out_W"].T.reshape(4, P, D).transpose(1, 0, 2).reshape(P, -1), "l0a_out_b": q["out_b"]}
    gates = np.zeros((2, 64, 2, 2, 4), np.float32)
    for j, n in enumerate(("Meta_W1", "Malpha_W1")):
        gates[j, :, :, j] = q[n].T.reshape(64, 4, 2).transpose(0, 2, 1)
    r["l0a_gates"] = gates.reshape(P, 16)
    vv = cat([q["Mk_W1"], q["Mv_W1"], q["Mvh_W2"].T], 1)
    r["l0a_vv"] = vv.reshape(4, P, 192).transpose(1, 0, 2).reshape(P, -1)
    r["l0a_conv"] = cat([q["conv_w"][:, 0, :], q["conv_b"][:, None]], 1)
    r["l0a_norms"] = cat([heads(q[n][None]).reshape(2, 256) for n in ("normk_g", "normk_b", "normq_g", "normq_b")], 1)
    i = np.arange(64)
    same, less, more = i[:, None] == i, i[:, None] < i, i[:, None] > i
    one = np.ones((64, 64))
    two = lambda m: np.tile(m, (2, 1))
    diag = lambda m: np.kron(np.eye(2), m)
    r["l0a_consts"] = cat([two(same), two(less), two(~less) * -1e30, diag(less), diag(more), diag(one),
                           np.tile(same, (2, 2))], 1).astype(np.float32)
    return r


def laid_out(a):
    import numpy as np
    cat, st = np.concatenate, np.stack
    side = lambda w: w.transpose(1, 0, 2).reshape(w.shape[1], -1)
    down = lambda w: w.reshape(w.shape[0], -1, P, D).transpose(2, 0, 1, 3).reshape(P, -1)
    two = lambda g, u: st([g, u], 2).transpose(1, 0, 2, 3).reshape(P, -1)
    r = {"x": a["x"].transpose(2, 0, 1), "tok_w": a["L0_tok_W"].T,
         "tok_cols": st([a["L0_tok_b"], a["L0_tok_gamma"], a["L0_tok_beta"]], 1)}
    q = {n[7:]: v for n, v in a.items() if n.startswith("L0_ffn_")}
    w1 = cat([q["expert_w1"], q["shared_w1"][None]]).reshape(17, D, 96, 2)
    r["l0f_w1"] = w1.transpose(1, 0, 3, 2).reshape(D, -1)
    r["l0f_w2"] = side(cat([q["expert_w2"], q["shared_w2"][None]]))
    r["l0f_b1"] = cat([q["expert_b1"], q["shared_b1"][None]]).reshape(17, 96, 2).transpose(1, 0, 2).reshape(96, -1)
    r["l0f_b2"] = cat([q["expert_b2"], q["shared_b2"][None]])
    r["l0f_scal"] = cat([q["expert_act"], q["shared_act"][None]]).reshape(-1)
    r["l0f_gate"], r["l0f_gate_b"] = q["gate_w"], np.tile(q["gate_b"], 3)
    q = {n[7:]: v for n, v in a.items() if n.startswith("L1_ffn_")}
    r["l1f_w1"], r["l1f_w2"], r["l1f_b2"] = side(q["w1"]), down(q["w2"]), q["b2"]
    r["l1f_b1"] = q["b1"].reshape(8, 4, P).transpose(2, 0, 1).reshape(P, -1)
    r["l1f_gate"], r["l1f_gate_b"] = q["router_w"], np.tile(q["router_b"], 3)
    q = {n[7:]: v for n, v in a.items() if n.startswith("L2_ffn_")}
    r["l2f_w1"], r["l2f_w2"], r["l2f_gate"] = two(q["W"], q["V"]), down(q["W2"]), q["Wg"]
    q = {n[7:]: v for n, v in a.items() if n.startswith("L3_ffn_")}
    r["l3f_w1"] = two(cat([q["w1"], q["sw1"][None]]), cat([q["w3"], q["sw3"][None]]))
    r["l3f_w2"] = down(cat([q["w2"], q["sw2"][None]]))
    r["l3f_gate"], r["l3f_gate_b"] = q["gate_w"].T, np.tile(q["biases"], 3)
    r.update(laid_out_delta({n[8:]: v for n, v in a.items() if n.startswith("L0_attn_")}))
    q = {n[8:]: v for n, v in a.items() if n.startswith("L1_attn_")}
    r["l1a_w"] = cat([q["w_qkv"][0:2 * D].T, q["w_out"].T], 1)
    r["l1a_out_b"] = q["b_out"]
    q = {n[8:]: v for n, v in a.items() if n.startswith("L3_attn_")}
    r["l3a_w"] = cat([q[c + "_w"].T for c in "qkvp"], 1)
    r["l3a_bn"] = st([q[c + n] for n in ("_b", "_g", "_beta", "_mu", "_var") for c in "qkvp"], 1)
    r["l3a_heads"] = np.kron(np.eye(8, dtype=np.float32), np.ones((16, 16), np.float32))
    qk = np.zeros((D, 2, 2, 4, 32), np.float32)
    kvw = a["L2_attn_kv_w"].T.reshape(D, 2, 8, 16)
    for j, m in enumerate((a["L2_attn_q_w"].T.reshape(D, 8, 16), kvw[:, 0])):
        qk[:, j, :, :, 0:16] = m.reshape(D, 2, 4, 16)
    r["l2a_w"] = cat([qk.reshape(D, -1), kvw[:, 1].reshape(D, -1)], 1)
    r["l2a_ones"] = (np.arange(P) % 32 == 16).astype(np.float32)[:, None]
    return {n: np.ascontiguousarray(v) for n, v in r.items()}


def program(nc, arrays, active=range(8)):
    W = {n: nc.dram_tensor("in_" + n, v.shape, mybir.dt.from_np(v.dtype), kind="ExternalInput").ap() for n, v in arrays.items()}
    out = nc.dram_tensor("out_dram", (B, L, D), F32, kind="ExternalOutput").ap()
    emit(nc, W, out, active)


def kernel(**inputs):
    import numpy as np
    import concourse.bacc as bacc
    from concourse.bass_utils import run_bass_kernel_spmd
    arrays = laid_out({n: np.asarray(v) for n, v in inputs.items()})
    nc = bacc.Bacc("TRN2", target_bir_lowering=False, num_devices=1)
    program(nc, arrays)
    return run_bass_kernel_spmd(nc, [{"in_" + n: v for n, v in arrays.items()}], core_ids=[0]).results[0]["out_dram"]
```
